# Optimizing a Trainium2 kernel written in Bass

```python
import numpy as np
import jax
import jax.numpy as jnp

def _softmax(x, axis=-1):
    return jax.nn.softmax(x, axis=axis)

def _gelu(x):
    return jax.nn.gelu(x, approximate=True)

def _silu(x):
    return jax.nn.silu(x)

def _sigmoid(x):
    return jax.nn.sigmoid(x)

def _layernorm(x, axis=-1, eps=1e-05):
    m = jnp.mean(x, axis=axis, keepdims=True)
    v = jnp.var(x, axis=axis, keepdims=True)
    return (x - m) / jnp.sqrt(v + eps)

def _scatter_add(tgt, idx, src, axis=0):
    return tgt.at[idx].add(src)

def _segment_sum(src, seg, n):
    return jax.ops.segment_sum(src, seg, n)
kernel_name = 'mk_flamingo_gated_d1_seqx_r8_c80437'

def setup_inputs(seed: int=0):
    np.random.seed(seed)
    _w = jnp.asarray

    def _rec_inputs():
        import jax
        import jax.numpy as jnp
        _rk = jax.random.key(seed)
        x = 7.22e-05 + 1 * jax.random.normal(jax.random.fold_in(_rk, 1), (4, 256, 128), jnp.float32)
        _lenS = 256 - jax.random.randint(jax.random.fold_in(_rk, 7), (4,), 0, max(1, 256 // 4) + 1, jnp.int32)
        _lenS2 = 512 - jax.random.randint(jax.random.fold_in(_rk, 8), (4,), 0, max(1, 512 // 4) + 1, jnp.int32)
        _ctx_1024P = jax.random.normal(jax.random.fold_in(_rk, 11), (4, 16, 128), jnp.float32)
        _ctx_1024c = jax.random.dirichlet(jax.random.fold_in(_rk, 511), 0.3 * jnp.ones((16,), jnp.float32), (4, 512))
        _ctx_1024t = jnp.einsum('bsk,bkd->bsd', _ctx_1024c, _ctx_1024P)
        _ctx_1024t = _ctx_1024t * jax.lax.rsqrt(jnp.mean(jnp.square(_ctx_1024t)) + 1e-12) * 0.953939
        ctx_1024 = 4.13588e-05 + 0.999923 * (_ctx_1024t + 0.3 * jax.random.normal(jax.random.fold_in(_rk, 611), (4, 512, 128), jnp.float32))
        _g = jax.random.normal(jax.random.fold_in(_rk, 9001), (2, 1), jnp.float32)
        _g = jnp.sign(_g) * jnp.maximum(jnp.abs(_g), 1.0) + (_g == 0) * 1.0
        g_xattn = _g[0]
        g_ffn = _g[1]
        return (x, ctx_1024, g_xattn, g_ffn)
    x, ctx_1024, g_xattn, g_ffn = _rec_inputs()

    def _L0_xattn_setup():
        import jax, jax.numpy as jnp
        import numpy as np
        N, L, E, H, D = (4, 256, 128, 16, 64)
        key = jax.random.key(seed)
        ks = jax.random.split(key, 8)
        s = 1.0 / np.sqrt(E)
        return {'Q': jax.random.normal(ks[0], (N, L, E), jnp.float32), 'K': jax.random.normal(ks[1], (N, L, E), jnp.float32), 'V': jax.random.normal(ks[2], (N, L, E), jnp.float32), 'Wq': jax.random.normal(ks[3], (H * D, E), jnp.float32) * s, 'bq': jnp.zeros((H * D,), jnp.float32), 'Wk': jax.random.normal(ks[4], (H * D, E), jnp.float32) * s, 'bk': jnp.zeros((H * D,), jnp.float32), 'Wv': jax.random.normal(ks[5], (H * D, E), jnp.float32) * s, 'bv': jnp.zeros((H * D,), jnp.float32), 'Wo': jax.random.normal(ks[6], (E, H * D), jnp.float32) * s, 'bo': jnp.zeros((E,), jnp.float32)}
    _L0_xattn_all = _L0_xattn_setup()
    _L0_xattn_in = {k: v for k, v in _L0_xattn_all.items() if k in ('Wq', 'bq', 'Wk', 'bk', 'Wv', 'bv', 'Wo', 'bo')}
    del _L0_xattn_all

    def _L0_ffn_setup():
        import jax, jax.numpy as jnp
        import numpy as np
        B, S, D, F, E, K = (4, 256, 128, 256, 8, 2)
        key = jax.random.key(seed)
        ks = jax.random.split(key, 9)
        sc = 0.02
        return {'hidden_states': jax.random.normal(ks[0], (B, S, D), jnp.float32), 'router_w': jax.random.normal(ks[1], (E, D), jnp.float32) * sc, 'w_gate': jax.random.normal(ks[2], (E, D, F), jnp.float32) * sc, 'w_up': jax.random.normal(ks[3], (E, D, F), jnp.float32) * sc, 'w_down': jax.random.normal(ks[4], (E, F, D), jnp.float32) * sc, 'sw_gate': jax.random.normal(ks[5], (D, F), jnp.float32) * sc, 'sw_up': jax.random.normal(ks[6], (D, F), jnp.float32) * sc, 'sw_down': jax.random.normal(ks[7], (F, D), jnp.float32) * sc, 'gate_w': jax.random.normal(ks[8], (1, D), jnp.float32) * sc}
    _L0_ffn_all = _L0_ffn_setup()
    _L0_ffn_in = {k: v for k, v in _L0_ffn_all.items() if k in ('router_w', 'w_gate', 'w_up', 'w_down', 'sw_gate', 'sw_up', 'sw_down', 'gate_w')}
    del _L0_ffn_all
    return {'x': x, 'ctx_1024': ctx_1024, 'g_xattn': g_xattn, 'g_ffn': g_ffn, 'L0_xattn_Wq': _L0_xattn_in['Wq'], 'L0_xattn_bq': _L0_xattn_in['bq'], 'L0_xattn_Wk': _L0_xattn_in['Wk'], 'L0_xattn_bk': _L0_xattn_in['bk'], 'L0_xattn_Wv': _L0_xattn_in['Wv'], 'L0_xattn_bv': _L0_xattn_in['bv'], 'L0_xattn_Wo': _L0_xattn_in['Wo'], 'L0_xattn_bo': _L0_xattn_in['bo'], 'L0_ffn_router_w': _L0_ffn_in['router_w'], 'L0_ffn_w_gate': _L0_ffn_in['w_gate'], 'L0_ffn_w_up': _L0_ffn_in['w_up'], 'L0_ffn_w_down': _L0_ffn_in['w_down'], 'L0_ffn_sw_gate': _L0_ffn_in['sw_gate'], 'L0_ffn_sw_up': _L0_ffn_in['sw_up'], 'L0_ffn_sw_down': _L0_ffn_in['sw_down'], 'L0_ffn_gate_w': _L0_ffn_in['gate_w']}

def reference(x, ctx_1024, g_xattn, g_ffn, L0_xattn_Wq, L0_xattn_bq, L0_xattn_Wk, L0_xattn_bk, L0_xattn_Wv, L0_xattn_bv, L0_xattn_Wo, L0_xattn_bo, L0_ffn_router_w, L0_ffn_w_gate, L0_ffn_w_up, L0_ffn_w_down, L0_ffn_sw_gate, L0_ffn_sw_up, L0_ffn_sw_down, L0_ffn_gate_w):
    import jax
    import jax.numpy as jnp

    def _L0_xattn_ref(Q, K, V, Wq, bq, Wk, bk, Wv, bv, Wo, bo):
        import jax, jax.numpy as jnp
        import numpy as np
        N, L, E, H, D = (4, 256, 128, 16, 64)
        n, lq, e = Q.shape
        lk = K.shape[1]
        q = (Q @ Wq.T + bq).reshape(n, lq, H, D)
        k = (K @ Wk.T + bk).reshape(n, lk, H, D)
        v = (V @ Wv.T + bv).reshape(n, lk, H, D)
        scores = jnp.einsum('nqhd,nkhd->nqkh', q, k) / jnp.sqrt(jnp.float32(D))
        attn = jax.nn.softmax(scores, axis=2)
        out = jnp.einsum('nqkh,nkhd->nqhd', attn, v)
        out = out.reshape(n, lq, H * D)
        return (out @ Wo.T + bo).reshape(n, lq, E)

    def _L0_ffn_ref(hidden_states, router_w, w_gate, w_up, w_down, sw_gate, sw_up, sw_down, gate_w):
        import jax, jax.numpy as jnp
        import numpy as np
        B, S, D, F, E, K = (4, 256, 128, 256, 8, 2)
        bsz, seq_len, d = hidden_states.shape
        x = hidden_states.reshape(-1, d)
        T = x.shape[0]
        n_exp = router_w.shape[0]
        logits = x @ router_w.T
        probs = jax.nn.softmax(logits, axis=-1)
        rw, sel = jax.lax.top_k(probs, K)
        cw = jnp.zeros((T, n_exp), x.dtype).at[jnp.arange(T)[:, None], sel].set(rw)
        g = jnp.einsum('td,edf->etf', x, w_gate)
        u = jnp.einsum('td,edf->etf', x, w_up)
        h = jax.nn.silu(g) * u
        y = jnp.einsum('etf,efd->etd', h, w_down)
        moe_out = jnp.einsum('te,etd->td', cw, y)
        shared = jax.nn.silu(x @ sw_gate) * (x @ sw_up) @ sw_down
        gate = jax.nn.sigmoid(x @ gate_w.T)
        out = moe_out + gate * shared
        return out.reshape(bsz, seq_len, d)
    x = x + jnp.tanh(g_xattn[0]) * _L0_xattn_ref(_layernorm(x, axis=-1), ctx_1024, ctx_1024, L0_xattn_Wq, L0_xattn_bq, L0_xattn_Wk, L0_xattn_bk, L0_xattn_Wv, L0_xattn_bv, L0_xattn_Wo, L0_xattn_bo)
    x = x + jnp.tanh(g_ffn[0]) * _L0_ffn_ref(_layernorm(x, axis=-1), L0_ffn_router_w, L0_ffn_w_gate, L0_ffn_w_up, L0_ffn_w_down, L0_ffn_sw_gate, L0_ffn_sw_up, L0_ffn_sw_down, L0_ffn_gate_w)
    return x

_drawn_inputs = setup_inputs


def setup_inputs(seed=0):
    import zlib

    import numpy as np

    out = dict(_drawn_inputs(seed))
    spreads = {'L0_xattn_bq': (0.0, 0.1),
     'L0_xattn_bk': (0.0, 0.8),
     'L0_xattn_bv': (0.0, 0.1),
     'L0_xattn_bo': (0.0, 0.1)}
    factors = {'L0_ffn_router_w': 8.0,
     'L0_ffn_w_gate': 8.0,
     'L0_ffn_w_up': 8.0,
     'L0_ffn_w_down': 8.0,
     'L0_ffn_sw_gate': 8.0,
     'L0_ffn_sw_up': 8.0,
     'L0_ffn_sw_down': 8.0,
     'L0_ffn_gate_w': 8.0}
    for name, (base, spread) in spreads.items():
        noise = np.random.default_rng([zlib.crc32(name.encode()), seed]).standard_normal(out[name].shape)
        drawn = base * np.exp(spread * noise) if base else spread * noise
        out[name] = jnp.asarray(drawn.astype(out[name].dtype))
    for name, factor in factors.items():
        out[name] = (out[name] * factor).astype(out[name].dtype)
    return out
```

```python
from contextlib import ExitStack

import concourse.bass as bass
from concourse import mybir

P = 128
ALU = mybir.AluOpType
ACT = mybir.ActivationFunctionType
AX = mybir.AxisListType
F32 = mybir.dt.float32
F16 = mybir.dt.float16
BF16 = mybir.dt.bfloat16

ACT_SCALE = 4.0
W_SCALE = 16.0
PROJ_SCALE = ACT_SCALE * W_SCALE
ROW_SCALE = 2048.0
EPS = 1e-5
NEVER = 4.0


def flamingo_block(nc, xs, ctxT, g_xattn, g_ffn, wqkv, bqk, bv, woT, bo, routerT, wffn, out):
    T, E = xs.shape
    HP = wqkv.shape[1]
    NB = 4
    L = T // NB
    S = ctxT.shape[1] // NB
    D = 64
    NT = T // P
    KT = S // P
    QT = L // P
    NE = wffn.shape[0]
    NR = NE - 1
    FT = 2
    UN = 2 * NB
    EXP_SCALE = 1.0 / (8.0 * PROJ_SCALE * PROJ_SCALE)
    HALF = T // 2
    assert E == P and L == 256 and S == 512 and T == 1024 and HP == 8 and NE == 9

    with ExitStack() as ctx:
        def sb(name, shape, dt):
            return ctx.enter_context(nc.sbuf_tensor(name, shape, dt))

        def sem(name):
            return ctx.enter_context(nc.semaphore(name))

        x_in = sb("x_in", [P, NT, P], F32)
        x_norm = sb("x_norm", [P, NT, P], F32)
        x_mid = sb("x_mid", [P, NT, P], F32)
        xT_hi = sb("xT_hi", [P, T], F16)
        xT_lo = sb("xT_lo", [P, T], F16)
        ctx_hi = sb("ctx_hi", [P, NB * S], F16)
        ctx_lo = sb("ctx_lo", [P, NB * S], F16)
        w_qkv = sb("w_qkv", [P, HP, 3 * P], F32)
        w_hi = sb("w_hi", [P, 2, 3 * P], F16)
        w_lo = sb("w_lo", [P, 2, 3 * P], F16)
        wo = sb("wo", [P, HP, P], F32)
        wo_hi = sb("wo_hi", [P, HP, P], F16)
        wo_lo = sb("wo_lo", [P, HP, P], F16)
        bias_qk = sb("bias_qk", [P, HP, 2], F32)
        bias_pair = sb("bias_pair", [P, 2, 2], F32)
        bias_v = sb("bias_v", [P, HP], F32)
        bo_row = sb("bo_row", [1, P], F32)
        g_col = sb("g_col", [P, 2], F32)
        tanh_g = sb("tanh_g", [P, 2], F32)
        q_hi = sb("q_hi", [P, T], F16)
        q_lo = sb("q_lo", [P, T], F16)
        k_hi = sb("k_hi", [P, NB * S], F16)
        k_lo = sb("k_lo", [P, NB * S], F16)
        k_both = sb("k_both", [P, 2, 2, NB * S], F16)
        k_row = sb("k_row", [P, 2, 2, NB * S], F16)
        q_twice = sb("q_twice", [P, 2, 2, T], F16)
        q_row = sb("q_row", [P, 2, 2, T], F16)
        v_sb = sb("v_sb", [P, 2, NB * KT, P], F32)
        probs = sb("probs", [P, 4, KT * L], F32)
        part_sum = sb("part_sum", [P, 2 * L], F32)
        prob_sum = sb("prob_sum", [P, 4, L], F32)
        max_cols = sb("max_cols", [P, 2, QT, P], BF16)
        neg_ident = sb("neg_ident", [P, P], BF16)
        ident = sb("ident", [P, P], F32)
        ones = sb("ones", [P, P], F32)
        ln_den = sb("ln_den", [P, L], F32)
        rec_den = sb("rec_den", [P, L], F32)
        den_rec = sb("den_rec", [P, L], F32)
        o_rec = sb("o_rec", [P, L], F32)
        o_norm = sb("o_norm", [P, 2, L], F32)
        oT_hi = sb("oT_hi", [P, HP, T], F16)
        oT_lo = sb("oT_lo", [P, HP, T], F16)
        stats = sb("stats", [P, NT, 6], F32)
        mean_var = sb("mean_var", [P, NT, 2], F32)
        ln_var = sb("ln_var", [P, NT], F32)
        rstd0 = sb("rstd0", [P, NT], F32)
        newton = sb("newton", [P, NT], F32)
        newton2 = sb("newton2", [P, NT], F32)
        rstd = sb("rstd", [P, NT], F32)
        eps_col = sb("eps_col", [P, 1], F32)
        bias_out = sb("bias_out", [P, P], F32)
        attn = sb("attn", [P, 4 * P], F32)
        router = sb("router", [P, NE], F32)
        router_hi = sb("router_hi", [P, NE], F16)
        router_lo = sb("router_lo", [P, NE], F16)
        logits = sb("logits", [P, NT, NE], F32)
        r_a = sb("r_a", [P, NT, NR], F32)
        r_b = sb("r_b", [P, NT, NR], F32)
        r_c = sb("r_c", [P, NT, NR], F32)
        prob_e = sb("prob_e", [P, NT, NR], F32)
        first_e = sb("first_e", [P, NT, NR], F32)
        order_e = sb("order_e", [P, NR], F32)
        r_m = sb("r_m", [P, NT], F32)
        r_s = sb("r_s", [P, NT], F32)
        gate_e = sb("gate_e", [P, NT], F32)
        mix = sb("mix", [P, NT, NE], F32)
        wf = sb("wf", [P, 2, 768], F32)

        ctx32 = probs[:, 0:2, :].rearrange("p a b -> p (a b)")
        bvw = v_sb[:, 0, 0:HP, :]
        silu = probs[:, 0, :].rearrange("p (a b) -> p a b", a=2)
        hid = probs[:, 1, :].rearrange("p (a b) -> p a b", a=2)
        hid_hi = k_both[:, 0, :, :].rearrange("p a (f t) -> p a f t", f=FT)
        hid_lo = k_both[:, 1, :, :].rearrange("p a (f t) -> p a f t", f=FT)
        wf_hi = k_hi[:, 0:1536].rearrange("p (a b) -> p a b", a=2)
        wf_lo = k_lo[:, 0:1536].rearrange("p (a b) -> p a b", a=2)

        banks = [ctx.enter_context(nc.psum_tensor(f"bank{i}", [P, 512], F32)) for i in range(8)]
        near = [banks[0], banks[1]]
        score = [banks[2], banks[3]]
        outs = [banks[4], banks[5]]
        misc = [banks[6], banks[7]]

        names = """x0_loaded x1_loaded ctx0_loaded ctx1_loaded ctx2_loaded ctx3_loaded w_first_loaded
        w_rest_loaded small_loaded wo_loaded wf0_loaded wf1_loaded consts
        pool_step stats_done var_ready ln_half rstd_done normed transposed xT_hi_done xT_done
        ctx_hi_done ctx_done w_hi_done w_done bias_done wo_done bias_prod bias_sum bias_out_done
        projected hi_done lo_done v_done q_moved k_moved near_done max_done shift_made shift_done
        scores_done probs_done sums_half sums_done pv_done ln_done rec_done div_half psum_read div_done
        oT_hi_done oT_done y_done attn_half attn_done router_done logits_done route route_exp route_act
        mix_done wf_hi_done wf_done gu_done silu_done hid_done hid_hi_done hid_lo_done down_done
        summed stored tanh_done router_hi_done""".split()
        s = {n: sem(n) for n in names}
        block = ctx.enter_context(nc.Block())

        SLOT_GROUPS = {1: [0, 1], 2: [2, 3], 3: [4], 4: [5], 5: [6], 6: [7], 7: [8, 9]}

        def loop_pairs(eng, body):
            body(0, 0, True, False)
            with eng.Fori(0, (HP - 2) // 2) as i:
                body(2 * i + 1, 1, False, False)
                body(2 * i + 2, 0, False, False)
            body(HP - 1, 1, False, True)

        def loop_experts(eng, body):
            body(0, 0, True, False)
            body(1, 1, False, False)
            with eng.Fori(0, (NE - 3) // 2) as i:
                body(2 * i + 2, 0, False, False)
                body(2 * i + 3, 1, False, False)
            body(NE - 1, 0, False, True)

        @block.sync
        def _(sp):
            xv = xs.rearrange("(t p) e -> p t e", p=P)
            for h in range(2):
                sp.dma_start(x_in[:, 4 * h:4 * h + 4, :], xv[:, 4 * h:4 * h + 4, :]).then_inc(s[f"x{h}_loaded"], 16)
            sp.dma_start(w_qkv[:, 0:1, :], wqkv[:, 0:1, :]).then_inc(s["w_first_loaded"], 16)
            for n in range(NB):
                sp.dma_start(ctx32[:, n * S:(n + 1) * S], ctxT[:, n * S:(n + 1) * S]).then_inc(s[f"ctx{n}_loaded"], 16)
            sp.dma_start(w_qkv[:, 1:HP, :], wqkv[:, 1:HP, :]).then_inc(s["w_rest_loaded"], 16)
            for e in range(2):
                sp.dma_start(wf[:, e, :], wffn[e]).then_inc(s[f"wf{e}_loaded"], 16)

            def move(hp1, par1, first):
                sp.wait_ge(s["lo_done"], 6 * hp1 + 2)
                if not first:
                    sp.wait_ge(s["scores_done"], 16 * hp1 - 16)
                for h in range(2):
                    rows = slice(D * h, D * h + D)
                    sp.dma_start(q_twice[0:D, par1, h, :], q_hi[rows, :]).then_inc(s["q_moved"], 16)
                    sp.dma_start(q_twice[D:P, par1, h, :], q_hi[rows, :]).then_inc(s["q_moved"], 16)
                    sp.dma_start(q_row[0:D, par1, h, :], q_lo[rows, :]).then_inc(s["q_moved"], 16)
                sp.wait_ge(s["lo_done"], 6 * hp1 + 6)
                for h in range(2):
                    rows = slice(D * h, D * h + D)
                    sp.dma_start(k_both[0:D, par1, h, :], k_hi[rows, :]).then_inc(s["k_moved"], 16)
                    sp.dma_start(k_both[D:P, par1, h, :], k_lo[rows, :]).then_inc(s["k_moved"], 16)
                    sp.dma_start(k_row[0:D, par1, h, :], k_hi[rows, :]).then_inc(s["k_moved"], 16)

            move(0, 0, True)
            move(1, 1, True)
            with sp.Fori(0, (HP - 2) // 2) as i:
                move(2 * i + 2, 0, False)
                move(2 * i + 3, 1, False)

            def load_expert(e, par):
                sp.wait_ge(s["wf_done"], 2 * e - 2)
                sp.dma_start(wf[:, par:par + 1, :], wffn[bass.ds(e, 1)].rearrange("e p f -> p e f")).then_inc(s[f"wf{par}_loaded"], 16)

            with sp.Fori(0, 3) as i:
                load_expert(2 * i + 2, 0)
                load_expert(2 * i + 3, 1)
            load_expert(NE - 1, 0)

            ov = out.rearrange("(t p) e -> p t e", p=P)
            for h in range(2):
                sp.wait_ge(s["summed"], 2 * NE - 1 + h)
                sp.dma_start(ov[:, 4 * h:4 * h + 4, :], x_mid[:, 4 * h:4 * h + 4, :]).then_inc(s["stored"], 16)
            sp.wait_ge(s["stored"], 32)

        @block.gpsimd
        def _(pool):
            for t, src in ((bias_qk[:, :, :], bqk), (bias_v, bv), (router, routerT), (bo_row, bo),
                           (g_col[:, 0:1], g_xattn), (g_col[:, 1:2], g_ffn)):
                pool.dma_start(t if isinstance(t, bass.AP) else t[:, :], src).then_inc(s["small_loaded"], 16)
            pool.dma_start(wo[:, :, :], woT.rearrange("(h p) e -> p h e", p=P)).then_inc(s["wo_loaded"], 16)
            pool.memset(ident[:, :], 0.0).then_inc(s["pool_step"], 1)
            pool.memset(neg_ident[:, :], 0.0).then_inc(s["pool_step"], 1)
            pool.wait_ge(s["pool_step"], 2)
            pool.affine_select(out=ident[:, :], in_=ident[:, :], compare_op=ALU.not_equal, fill=1.0, base=0,
                               pattern=[[-1, P]], channel_multiplier=1).then_inc(s["consts"], 1)
            pool.affine_select(out=neg_ident[:, :], in_=neg_ident[:, :], compare_op=ALU.not_equal,
                               fill=-1.0 / ROW_SCALE, base=0, pattern=[[-1, P]], channel_multiplier=1).then_inc(s["consts"], 1)
            pool.memset(max_cols[:, :, :, :], 0.0).then_inc(s["consts"], 1)
            pool.memset(ones[:, :], 1.0).then_inc(s["consts"], 1)
            for par in range(2):
                pool.wait_ge(s["consts"], 4 + 2 * par)
                pool.memset(q_row[D:P, par, :, :].bitcast(F32), 0.0).then_inc(s["consts"], 1)
                pool.wait_ge(s["consts"], 5 + 2 * par)
                pool.memset(k_row[D:P, par, :, :].bitcast(F32), 0.0).then_inc(s["pool_step"], 1)
                pool.wait_ge(s["pool_step"], 3 + par)
                pool.memset(k_row[D:D + 1, par, :, :], ROW_SCALE).then_inc(s["consts"], 1)
            pool.wait_ge(s["consts"], 8)
            for e in range(NR):
                last = pool.memset(order_e[:, e:e + 1], float(NR - e))
            last.then_inc(s["consts"], 1)
            pool.wait_ge(s["wo_loaded"], 16)
            pool.tensor_scalar(wo[:, :, :], wo[:, :, :], W_SCALE, None, ALU.mult).then_inc(s["wo_done"], 1)
            pool.wait_ge(s["wo_done"], 1)
            pool.tensor_scalar(wo_hi[:, :, :], wo[:, :, :], 1.0, None, ALU.mult).then_inc(s["wo_done"], 1)
            pool.wait_ge(s["wo_done"], 2)
            pool.tensor_tensor(wo_lo[:, :, :], wo[:, :, :], wo_hi[:, :, :], ALU.subtract).then_inc(s["wo_done"], 1)

            def low_o(m, hp, n):
                pool.wait_ge(s["oT_hi_done"], m + 1)
                pool.tensor_tensor(oT_lo[:, bass.ds(hp, 1), n * L:(n + 1) * L], o_norm[:, n % 2:n % 2 + 1, :],
                                   oT_hi[:, bass.ds(hp, 1), n * L:(n + 1) * L], ALU.subtract).then_inc(s["oT_done"], 1)

            def body(hp, par, first, last):
                for u in range(UN):
                    U, n, slot = hp * UN + u, u // 2, (u // 2) % 2 * 2 + u % 2
                    if not first or u >= 1:
                        pool.wait_ge(s["sums_done"], U)
                    pool.wait_ge(s["probs_done"], 2 * U + 2)
                    pool.tensor_tensor(part_sum[:, :], probs[:, slot, 0:2 * L], probs[:, slot, 2 * L:4 * L],
                                       ALU.add).then_inc(s["sums_half"], 1)
                    pool.wait_ge(s["sums_half"], U + 1)
                    pool.tensor_tensor(prob_sum[:, slot, :], part_sum[:, 0:L], part_sum[:, L:2 * L],
                                       ALU.add).then_inc(s["sums_done"], 1)
                    if u % 2 == 1:
                        if n >= 2:
                            low_o(4 * hp + n - 2, hp, n - 2)
                        elif not first:
                            low_o(4 * hp + n - 2, hp - 1, n + 2)

            loop_pairs(pool, body)
            low_o(4 * HP - 2, HP - 1, 2)
            low_o(4 * HP - 1, HP - 1, 3)

            def expert(e, par, first, last):
                for c in range(4):
                    C, tc, ft = 4 * e + c, c // 2, c % 2
                    pool.wait_ge(s["hid_hi_done"], C + 1)
                    pool.tensor_tensor(hid_lo[:, par, ft, tc * 512:(tc + 1) * 512], hid[:, c % 2, :],
                                       hid_hi[:, par, ft, tc * 512:(tc + 1) * 512], ALU.subtract).then_inc(s["hid_lo_done"], 1)

            loop_experts(pool, expert)

        @block.scalar
        def _(act):
            act.wait_ge(s["small_loaded"], 96)
            act.activation(tanh_g[:, :], g_col[:, :], ACT.Tanh).then_inc(s["tanh_done"], 1)
            act.preload_act_table_set("natural_log_exp_and_others")
            act.wait_ge(s["w_first_loaded"], 16)

            def split_w(hp, par):
                act.activation(w_hi[:, par:par + 1, :], w_qkv[:, bass.ds(hp, 1), :], ACT.Copy,
                               scale=W_SCALE).then_inc(s["w_hi_done"], 1)

            split_w(0, 0)
            for n in range(NB):
                act.wait_ge(s[f"ctx{n}_loaded"], 16)
                act.activation(ctx_hi[:, n * S:(n + 1) * S], ctx32[:, n * S:(n + 1) * S], ACT.Copy,
                               scale=ACT_SCALE).then_inc(s["ctx_hi_done"], 1)

            def rstd_guess(half, at):
                act.wait_ge(s["stats_done"], at + 1)
                act.activation(ln_var[:, 4 * half:4 * half + 4], mean_var[:, 4 * half:4 * half + 4, 1], ACT.Ln,
                               bias=eps_col[:, 0:1]).then_inc(s["ln_half"], 1)
                act.wait_ge(s["ln_half"], at + 1)
                act.activation(rstd0[:, 4 * half:4 * half + 4], ln_var[:, 4 * half:4 * half + 4], ACT.Exp,
                               scale=-0.5).then_inc(s["var_ready"], 1)

            def high_x(half, at):
                act.wait_ge(s["transposed"], at + 1)
                act.activation(xT_hi[:, half * HALF:(half + 1) * HALF], misc[half][:, :], ACT.Copy).then_inc(s["xT_hi_done"], 1)

            for half in range(2):
                rstd_guess(half, half)
            for half in range(2):
                high_x(half, half)

            def evacuate(hp1, par1, g, first):
                act.wait_ge(s["projected"], 10 * hp1 + g + 1)
                if g == 0:
                    act.wait_ge(s["bias_done"], hp1 + 1)
                if g < 2:
                    if g == 0 and not first:
                        act.wait_ge(s["q_moved"], 96 * hp1)
                    act.activation(q_hi[:, g * 512:(g + 1) * 512], misc[g % 2][:, :], ACT.Identity,
                                   bias=bias_pair[:, par1, 0:1]).then_inc(s["hi_done"], 1)
                elif g < 6:
                    if g == 2 and not first:
                        act.wait_ge(s["k_moved"], 96 * hp1)
                    act.activation(k_hi[:, (g - 2) * 512:(g - 1) * 512], misc[g % 2][:, :], ACT.Identity,
                                   bias=bias_pair[:, par1, 1:2]).then_inc(s["hi_done"], 1)
                else:
                    act.activation(v_sb[:, par1, (g - 6) * KT:(g - 5) * KT, :], misc[g % 2][:, :].rearrange("p (a b) -> p a b", a=KT),
                                   ACT.Copy).then_inc(s["v_done"], 1)

            def place_shift(U, par, n, h):
                act.wait_ge(s["shift_made"], U + 1)
                for qt in range(QT):
                    last = act.activation(q_row[D:D + 1, par, h, n * L + qt * P:n * L + (qt + 1) * P],
                                          near[qt][D:D + 1, 0:P], ACT.Copy)
                last.then_inc(s["shift_done"], 1)

            def reciprocal_guess(m, n):
                act.wait_ge(s["pv_done"], m + 1)
                act.activation(ln_den[:, :], outs[n % 2][:, L:2 * L], ACT.Ln).then_inc(s["ln_done"], 1)
                act.wait_ge(s["ln_done"], m + 1)
                act.activation(rec_den[:, :], ln_den[:, :], ACT.Exp, scale=-1.0).then_inc(s["rec_done"], 1)

            def high_o(m, hp, n):
                act.wait_ge(s["div_done"], m + 1)
                act.activation(oT_hi[:, bass.ds(hp, 1), n * L:(n + 1) * L], o_norm[:, n % 2:n % 2 + 1, :],
                               ACT.Copy).then_inc(s["oT_hi_done"], 1)

            for g in range(10):
                evacuate(0, 0, g, True)
            act.wait_ge(s["consts"], 5)
            place_shift(0, 0, 0, 0)

            def body(hp, par, first, last):
                for u in range(UN):
                    U, n, h = hp * UN + u, u // 2, u % 2
                    slot = n % 2 * 2 + h
                    if u == UN - 1 and first:
                        act.wait_ge(s["consts"], 7)
                    if u == 0 and not last:
                        if first:
                            act.wait_ge(s["w_rest_loaded"], 16)
                        split_w(hp + 1, 1 - par)
                    if u < UN - 1:
                        place_shift(U + 1, par, (u + 1) // 2, (u + 1) % 2)
                    elif not last:
                        place_shift(U + 1, 1 - par, 0, 0)
                    act.wait_ge(s["scores_done"], 2 * U + 1)
                    if not first or n >= 2:
                        act.wait_ge(s["pv_done"], 4 * hp + n - 1)
                    act.activation(probs[:, slot, 0:512], score[0][:, :], ACT.Exp, scale=EXP_SCALE).then_inc(s["probs_done"], 1)
                    if not last:
                        for g in SLOT_GROUPS.get(u, []):
                            evacuate(hp + 1, 1 - par, g, False)
                    act.wait_ge(s["scores_done"], 2 * U + 2)
                    act.activation(probs[:, slot, 512:1024], score[1][:, :], ACT.Exp, scale=EXP_SCALE).then_inc(s["probs_done"], 1)
                    if not first or n >= 2:
                        if h == 0:
                            reciprocal_guess(4 * hp + n - 2, n % 2)
                        elif n >= 2:
                            high_o(4 * hp + n - 2, hp, n - 2)
                        else:
                            high_o(4 * hp + n - 2, hp - 1, n + 2)

            loop_pairs(act, body)
            reciprocal_guess(4 * HP - 2, 0)
            high_o(4 * HP - 2, HP - 1, 2)
            reciprocal_guess(4 * HP - 1, 1)
            high_o(4 * HP - 1, HP - 1, 3)

            act.wait_ge(s["small_loaded"], 96)
            act.activation(router_hi[:, :], router[:, :], ACT.Copy, scale=W_SCALE).then_inc(s["router_hi_done"], 1)
            for half in range(2):
                rstd_guess(half, 2 + half)
            for half in range(2):
                high_x(half, 2 + half)

            act.wait_ge(s["route_exp"], 1)
            act.activation(r_b[:, :, :], r_a[:, :, :], ACT.Exp).then_inc(s["route_act"], 1)
            act.activation(gate_e[:, :], logits[:, :, NR], ACT.Exp, scale=-1.0).then_inc(s["route_act"], 1)

            def split_gate_up(e, par):
                act.wait_ge(s[f"wf{par}_loaded"], 8 * (e - par) + 16)
                act.activation(wf_hi[:, par, 0:512], wf[:, par, 0:512], ACT.Copy, scale=W_SCALE).then_inc(s["wf_hi_done"], 1)

            def split_down(par):
                act.activation(wf_hi[:, par, 512:768], wf[:, par, 512:768], ACT.Copy, scale=W_SCALE).then_inc(s["wf_hi_done"], 1)

            split_gate_up(0, 0)
            split_down(0)

            def high_hidden(C, par, c):
                act.wait_ge(s["hid_done"], C + 1)
                act.activation(hid_hi[:, par, c % 2, (c // 2) * 512:(c // 2 + 1) * 512], hid[:, c % 2, :],
                               ACT.Copy).then_inc(s["hid_hi_done"], 1)

            def expert(e, par, first, last):
                for c in range(4):
                    C = 4 * e + c
                    act.wait_ge(s["gu_done"], C + 1)
                    if not first or c >= 2:
                        act.wait_ge(s["hid_done"], C - 1)
                    act.activation(silu[:, c % 2, :], score[c % 2][:, :], ACT.Silu, scale=1.0 / PROJ_SCALE).then_inc(s["silu_done"], 1)
                    if c == 0:
                        if not first:
                            high_hidden(C - 1, 1 - par, 3)
                    else:
                        if c == 1 and not first:
                            act.wait_ge(s["down_done"], 2 * e - 2)
                        high_hidden(C - 1, par, c - 1)
                    if c == 1 and not last:
                        split_gate_up(e + 1, 1 - par)
                    if c == 3 and not last:
                        if not first:
                            act.wait_ge(s["down_done"], 2 * e)
                        split_down(1 - par)

            loop_experts(act, expert)
            high_hidden(4 * NE - 1, 0, 3)

        @block.vector
        def _(dve):
            dve.memset(eps_col[:, :], EPS)

            def layer_stats(src, half, at):
                for t in range(4 * half, 4 * half + 4):
                    dve.bn_stats(stats[:, t, :], src[:, t, :]).then_inc(s["attn_half"], 1)
                for j, t in enumerate(range(4 * half, 4 * half + 4)):
                    dve.wait_ge(s["attn_half"], 4 * at + j + 1)
                    last = dve.bn_aggr(mean_var[:, t, :], stats[:, t, :])
                last.then_inc(s["stats_done"], 1)

            def layer_norm(src, half, at):
                hs = slice(4 * half, 4 * half + 4)
                step = 4 * at
                dve.wait_ge(s["var_ready"], at + 1)
                dve.wait_ge(s["stats_done"], at + 1)
                dve.scalar_tensor_tensor(newton[:, hs], mean_var[:, hs, 1], EPS, rstd0[:, hs], ALU.add,
                                         ALU.mult).then_inc(s["rstd_done"], 1)
                dve.wait_ge(s["rstd_done"], step + 1)
                dve.tensor_tensor(newton2[:, hs], newton[:, hs], rstd0[:, hs], ALU.mult).then_inc(s["rstd_done"], 1)
                dve.wait_ge(s["rstd_done"], step + 2)
                dve.tensor_scalar(newton[:, hs], newton2[:, hs], -0.5 * ACT_SCALE, 1.5 * ACT_SCALE, ALU.mult,
                                  ALU.add).then_inc(s["rstd_done"], 1)
                dve.wait_ge(s["rstd_done"], step + 3)
                dve.tensor_tensor(rstd[:, hs], newton[:, hs], rstd0[:, hs], ALU.mult).then_inc(s["rstd_done"], 1)
                dve.wait_ge(s["rstd_done"], step + 4)
                for t in range(4 * half, 4 * half + 4):
                    last = dve.tensor_scalar(x_norm[:, t, :], src[:, t, :], mean_var[:, t, 0:1], rstd[:, t:t + 1],
                                             ALU.subtract, ALU.mult)
                last.then_inc(s["normed"], 1)

            def low_x(half, at):
                dve.wait_ge(s["xT_hi_done"], at + 1)
                dve.tensor_tensor(xT_lo[:, half * HALF:(half + 1) * HALF], misc[half][:, :],
                                  xT_hi[:, half * HALF:(half + 1) * HALF], ALU.subtract).then_inc(s["xT_done"], 1)

            def low_w(hp, par):
                dve.tensor_scalar(bias_pair[:, par:par + 1, :], bias_qk[:, bass.ds(hp, 1), :], PROJ_SCALE, None,
                                  ALU.mult).then_inc(s["bias_done"], 1)
                dve.wait_ge(s["w_hi_done"], hp + 1)
                dve.scalar_tensor_tensor(w_lo[:, par:par + 1, :], w_qkv[:, bass.ds(hp, 1), :], W_SCALE,
                                         w_hi[:, par:par + 1, :], ALU.mult, ALU.subtract).then_inc(s["w_done"], 1)

            for half in range(2):
                dve.wait_ge(s[f"x{half}_loaded"], 16)
                layer_stats(x_in, half, half)
            dve.wait_ge(s["small_loaded"], 96)
            low_w(0, 0)
            for half in range(2):
                layer_norm(x_in, half, half)
            for half in range(2):
                low_x(half, half)
            for n in range(NB):
                dve.wait_ge(s["ctx_hi_done"], n + 1)
                dve.scalar_tensor_tensor(ctx_lo[:, n * S:(n + 1) * S], ctx32[:, n * S:(n + 1) * S], ACT_SCALE,
                                         ctx_hi[:, n * S:(n + 1) * S], ALU.mult, ALU.subtract).then_inc(s["ctx_done"], 1)

            def low_part(hp1, par1, g):
                dve.wait_ge(s["hi_done"], 6 * hp1 + g + 1)
                if g == 0:
                    dve.wait_ge(s["bias_done"], hp1 + 1)
                if g < 2:
                    lo, hi, b, at = q_lo, q_hi, bias_pair[:, par1, 0:1], g * 512
                else:
                    lo, hi, b, at = k_lo, k_hi, bias_pair[:, par1, 1:2], (g - 2) * 512
                dve.scalar_tensor_tensor(lo[:, at:at + 512], misc[g % 2][:, :], b, hi[:, at:at + 512],
                                         ALU.add, ALU.subtract).then_inc(s["lo_done"], 1)

            def take_max(U, u, first):
                for qt in range(QT):
                    dve.wait_ge(s["near_done"], 2 * U + qt + 1)
                    if not first and qt == 0:
                        dve.wait_ge(s["shift_made"], U - 1)
                    dve.tensor_reduce(max_cols[:, u % 2, qt, D:D + 1], near[qt][:, :], AX.X, ALU.max).then_inc(s["max_done"], 1)

            def divide(m, n):
                dve.wait_ge(s["rec_done"], m + 1)
                dve.tensor_tensor(den_rec[:, :], outs[n % 2][:, L:2 * L], rec_den[:, :], ALU.mult).then_inc(s["div_half"], 1)
                dve.tensor_tensor(o_rec[:, :], outs[n % 2][:, 0:L], rec_den[:, :], ALU.mult).then_inc(s["psum_read"], 1)
                dve.wait_ge(s["div_half"], m + 1)
                dve.wait_ge(s["psum_read"], m + 1)
                dve.scalar_tensor_tensor(o_norm[:, n % 2, :], den_rec[:, :], -2.0, o_rec[:, :], ALU.add,
                                         ALU.mult).then_inc(s["div_done"], 1)

            for g in range(6):
                low_part(0, 0, g)
            dve.wait_ge(s["consts"], 4)
            take_max(0, 0, True)
            take_max(1, 1, True)

            def body(hp, par, first, last):
                for u in range(UN):
                    U, n, h = hp * UN + u, u // 2, u % 2
                    if u == 0 and not last:
                        low_w(hp + 1, 1 - par)
                    if not last:
                        for g in SLOT_GROUPS.get(u, []):
                            if g < 6:
                                low_part(hp + 1, 1 - par, g)
                    if not (last and u >= UN - 2):
                        take_max(U + 2, u, False)
                    if h == 0 and (not first or n >= 2):
                        if not first:
                            dve.wait_ge(s["oT_done"], 4 * hp + n - 3)
                        divide(4 * hp + n - 2, n % 2)

            loop_pairs(dve, body)
            dve.wait_ge(s["oT_done"], 4 * HP - 3)
            divide(4 * HP - 2, 0)
            dve.wait_ge(s["oT_done"], 4 * HP - 2)
            divide(4 * HP - 1, 1)

            dve.wait_ge(s["wo_done"], 3)
            dve.wait_ge(s["pv_done"], 4 * HP)
            dve.tensor_tensor(bvw, wo[:, :, :], bias_v[:, :].unsqueeze(2).broadcast_to([P, HP, P]), ALU.mult).then_inc(s["bias_prod"], 1)
            dve.tensor_scalar(bo_row[:, :], bo_row[:, :], W_SCALE, None, ALU.mult).then_inc(s["bias_prod"], 1)
            dve.wait_ge(s["bias_sum"], 1)
            dve.tensor_scalar(bias_out[:, :], outs[0][:, 0:P], 1.0 / W_SCALE, None, ALU.mult).then_inc(s["bias_out_done"], 1)
            dve.wait_ge(s["bias_out_done"], 1)
            dve.wait_ge(s["tanh_done"], 1)
            for half in range(2):
                hs = slice(4 * half, 4 * half + 4)
                dve.wait_ge(s["y_done"], half + 1)
                if half:
                    dve.wait_ge(s["attn_done"], half)
                dve.scalar_tensor_tensor(attn[:, :].rearrange("p (a b) -> p a b", a=4), near[half][:, :].rearrange("p (a b) -> p a b", a=4),
                                         -1.0 / (PROJ_SCALE * W_SCALE), bias_out[:, :].unsqueeze(1).broadcast_to([P, 4, P]),
                                         ALU.mult, ALU.add).then_inc(s["route"], 1)
                dve.wait_ge(s["route"], half + 1)
                dve.scalar_tensor_tensor(x_mid[:, hs, :].rearrange("p a b -> p (a b)"), attn[:, :], tanh_g[:, 0:1],
                                         x_in[:, hs, :].rearrange("p a b -> p (a b)"), ALU.mult, ALU.add).then_inc(s["attn_done"], 1)
                dve.wait_ge(s["attn_done"], half + 1)
                layer_stats(x_mid, half, 2 + half)
            for half in range(2):
                layer_norm(x_mid, half, 2 + half)
            dve.wait_ge(s["router_hi_done"], 1)
            dve.scalar_tensor_tensor(router_lo[:, :], router[:, :], W_SCALE, router_hi[:, :], ALU.mult,
                                     ALU.subtract).then_inc(s["router_done"], 1)
            for half in range(2):
                low_x(half, 2 + half)

            def low_gate_up(e, par):
                dve.wait_ge(s["wf_hi_done"], 2 * e + 1)
                dve.scalar_tensor_tensor(wf_lo[:, par, 0:512], wf[:, par, 0:512], W_SCALE, wf_hi[:, par, 0:512],
                                         ALU.mult, ALU.subtract).then_inc(s["wf_done"], 1)

            def low_down(e, par):
                dve.wait_ge(s["wf_hi_done"], 2 * e + 2)
                dve.scalar_tensor_tensor(wf_lo[:, par, 512:768], wf[:, par, 512:768], W_SCALE, wf_hi[:, par, 512:768],
                                         ALU.mult, ALU.subtract).then_inc(s["wf_done"], 1)

            count = [2]

            def link(ins):
                count[0] += 1
                ins.then_inc(s["route"], 1)
                dve.wait_ge(s["route"], count[0])

            def over_experts(col):
                return col[:, :].unsqueeze(2).broadcast_to([P, NT, NR])

            order = order_e[:, :].unsqueeze(1).broadcast_to([P, NT, NR])
            dve.wait_ge(s["logits_done"], 1)
            link(dve.tensor_scalar(logits[:, :, :], banks[0][:, 0:16 * NT].rearrange("p (t e) -> p t e", e=16)[:, :, 0:NE],
                                   1.0 / PROJ_SCALE, None, ALU.mult))
            link(dve.tensor_reduce(r_m[:, :], logits[:, :, 0:NR], AX.X, ALU.max))
            dve.tensor_tensor(r_a[:, :, :], logits[:, :, 0:NR], over_experts(r_m), ALU.subtract).then_inc(s["route_exp"], 1)
            low_gate_up(0, 0)
            low_down(0, 0)
            dve.wait_ge(s["route_act"], 2)
            link(dve.tensor_reduce(r_s[:, :], r_b[:, :, :], AX.X, ALU.add))
            link(dve.reciprocal(r_m[:, :], r_s[:, :]))
            link(dve.tensor_tensor(prob_e[:, :, :], r_b[:, :, :], over_experts(r_m), ALU.mult))
            dve.wait_ge(s["consts"], 9)

            def pick(dst, src):
                link(dve.tensor_reduce(r_m[:, :], src[:, :, :], AX.X, ALU.max))
                link(dve.tensor_tensor(r_a[:, :, :], src[:, :, :], over_experts(r_m), ALU.is_ge))
                link(dve.tensor_tensor(r_b[:, :, :], r_a[:, :, :], order, ALU.mult))
                link(dve.tensor_reduce(r_s[:, :], r_b[:, :, :], AX.X, ALU.max))
                link(dve.tensor_tensor(dst[:, :, :], r_b[:, :, :], over_experts(r_s), ALU.is_equal))

            pick(first_e, prob_e)
            link(dve.scalar_tensor_tensor(r_c[:, :, :], first_e[:, :, :], -NEVER, prob_e[:, :, :], ALU.mult, ALU.add))
            pick(r_a, r_c)
            link(dve.tensor_tensor(r_b[:, :, :], r_a[:, :, :], first_e[:, :, :], ALU.add))
            link(dve.tensor_tensor(mix[:, :, 0:NR], r_b[:, :, :], prob_e[:, :, :], ALU.mult))
            link(dve.tensor_scalar(r_s[:, :], gate_e[:, :], 1.0, None, ALU.add))
            link(dve.reciprocal(mix[:, :, NR], r_s[:, :]))
            dve.tensor_scalar(mix[:, :, :], mix[:, :, :], tanh_g[:, 1:2], 1.0 / (PROJ_SCALE * W_SCALE), ALU.mult,
                              ALU.mult).then_inc(s["mix_done"], 1)
            dve.wait_ge(s["mix_done"], 1)

            def combine(at, e, yb):
                dve.wait_ge(s["down_done"], at + 1)
                for t in range(4):
                    last = dve.scalar_tensor_tensor(x_mid[:, 4 * yb + t, :], misc[yb][:, t * P:(t + 1) * P],
                                                    mix[:, 4 * yb + t, bass.ds(e, 1)], x_mid[:, 4 * yb + t, :],
                                                    ALU.mult, ALU.add)
                last.then_inc(s["summed"], 1)

            def expert(e, par, first, last):
                for c in range(4):
                    C = 4 * e + c
                    dve.wait_ge(s["silu_done"], C + 1)
                    if not first or c >= 2:
                        dve.wait_ge(s["hid_lo_done"], C - 1)
                    dve.tensor_tensor(hid[:, c % 2, :], outs[c % 2][:, :], silu[:, c % 2, :], ALU.mult).then_inc(s["hid_done"], 1)
                    if not first and c >= 2:
                        combine(2 * e - 2 + c - 2, e - 1, c - 2)
                    if c == 1 and not last:
                        low_gate_up(e + 1, 1 - par)
                    if c == 3 and not last:
                        low_down(e + 1, 1 - par)

            loop_experts(dve, expert)
            combine(2 * NE - 2, NE - 1, 0)
            combine(2 * NE - 1, NE - 1, 1)

        @block.tensor
        def _(pe):
            def three(out_ap, lhs_hi, lhs_lo, rhs_hi, rhs_lo, start=True, stop=True):
                pe.matmul(out_ap, lhs_hi, rhs_hi, start=start, stop=False)
                pe.matmul(out_ap, lhs_hi, rhs_lo, start=False, stop=False)
                return pe.matmul(out_ap, lhs_lo, rhs_hi, start=False, stop=stop)

            def turn_x(half, at):
                pe.wait_ge(s["normed"], at + 1)
                for j in range(4):
                    last = pe.transpose(misc[half][:, j * P:(j + 1) * P], x_norm[:, 4 * half + j, :], ident[:, :])
                last.then_inc(s["transposed"], 1)

            def project(hp1, par1, g, first):
                if g == 0:
                    pe.wait_ge(s["w_done"], hp1 + 1)
                if g >= 8:
                    pe.wait_ge(s["v_done"], 4 * hp1 + g - 7)
                elif g >= 2:
                    pe.wait_ge(s["lo_done"], 6 * hp1 + g - 1)
                elif not first:
                    pe.wait_ge(s["v_done"], 4 * hp1 + g - 1)
                out_ap = misc[g % 2]
                if g < 2:
                    cols = slice(g * 512, (g + 1) * 512)
                    last = three(out_ap[:, :], w_hi[:, par1, 0:P], w_lo[:, par1, 0:P], xT_hi[:, cols], xT_lo[:, cols])
                elif g < 6:
                    if first:
                        pe.wait_ge(s["ctx_done"], g - 1)
                    cols = slice((g - 2) * 512, (g - 1) * 512)
                    last = three(out_ap[:, :], w_hi[:, par1, P:2 * P], w_lo[:, par1, P:2 * P], ctx_hi[:, cols], ctx_lo[:, cols])
                else:
                    for kt in range(KT):
                        cols = slice(((g - 6) * KT + kt) * P, ((g - 6) * KT + kt + 1) * P)
                        last = three(out_ap[:, kt * P:(kt + 1) * P], ctx_hi[:, cols], ctx_lo[:, cols],
                                     w_hi[:, par1, 2 * P:3 * P], w_lo[:, par1, 2 * P:3 * P])
                last.then_inc(s["projected"], 1)

            def near_scores(U, u, par):
                n, h = u // 2, u % 2
                for qt in range(QT):
                    cols = slice(n * L + qt * P, n * L + (qt + 1) * P)
                    pe.matmul(near[qt][:, :], q_twice[:, par, h, cols], k_both[:, par, h, n * S:(n + 1) * S],
                              start=True, stop=True).then_inc(s["near_done"], 1)

            def turn_max(U, u):
                pe.wait_ge(s["max_done"], 2 * U + 2)
                for qt in range(QT):
                    last = pe.matmul(near[qt][:, 0:P], max_cols[:, u % 2, qt, :], neg_ident[:, :], start=True, stop=True)
                last.then_inc(s["shift_made"], 1)

            def scores(U, u, par, half):
                n, h = u // 2, u % 2
                qs = slice(n * L, (n + 1) * L)
                for j in range(2):
                    kt = 2 * half + j
                    ks = slice(n * S + kt * P, n * S + (kt + 1) * P)
                    pe.matmul(score[half][:, j * L:(j + 1) * L], k_both[:, par, h, ks], q_twice[:, par, h, qs],
                              start=True, stop=False)
                    last = pe.matmul(score[half][:, j * L:(j + 1) * L], k_row[:, par, h, ks], q_row[:, par, h, qs],
                                     start=False, stop=True)
                last.then_inc(s["scores_done"], 1)

            def weigh_values(m, n, vpar, part, guard):
                bank = outs[n % 2]
                if part == 0:
                    pe.wait_ge(s["probs_done"], 4 * m + 4)
                    if guard:
                        pe.wait_ge(s["psum_read"], m - 1)
                for kt in (0, 1) if part == 0 else (2, 3):
                    for h in range(2):
                        pe.matmul(bank[D * h:D * h + D, 0:L], v_sb[:, vpar, n * KT + kt, D * h:D * h + D],
                                  probs[:, n % 2 * 2 + h, kt * L:(kt + 1) * L], start=(kt == 0), stop=(kt == 3))
                if part == 1:
                    pe.wait_ge(s["sums_done"], 2 * m + 2)
                    for h in range(2):
                        last = pe.matmul(bank[D * h:D * h + D, L:2 * L], ones[:, 0:D], prob_sum[:, n % 2 * 2 + h, :],
                                         start=True, stop=True)
                    last.then_inc(s["pv_done"], 1)

            pe.wait_ge(s["consts"], 1)
            for half in range(2):
                turn_x(half, half)
            pe.wait_ge(s["xT_done"], 2)
            for g in range(10):
                project(0, 0, g, True)
            pe.wait_ge(s["consts"], 6)
            pe.wait_ge(s["q_moved"], 96)
            pe.wait_ge(s["k_moved"], 96)
            near_scores(0, 0, 0)
            turn_max(0, 0)
            pe.wait_ge(s["shift_done"], 1)
            near_scores(1, 1, 0)

            def body(hp, par, first, last):
                for u in range(UN):
                    U, n, h = hp * UN + u, u // 2, u % 2
                    if not (last and u == UN - 1):
                        turn_max(U + 1, u + 1)
                    pe.wait_ge(s["shift_done"], U + 1)
                    if not first or u >= 1:
                        pe.wait_ge(s["probs_done"], 2 * U - 1)
                    scores(U, u, par, 0)
                    if not last:
                        for g in SLOT_GROUPS.get(u, []):
                            project(hp + 1, 1 - par, g, False)
                    if not (last and u >= UN - 2):
                        pe.wait_ge(s["shift_done"], U + 2)
                        if u == UN - 2:
                            if first:
                                pe.wait_ge(s["consts"], 8)
                            pe.wait_ge(s["q_moved"], 96 * hp + 192)
                            pe.wait_ge(s["k_moved"], 96 * hp + 192)
                        near_scores(U + 2, (u + 2) % UN, par if u < UN - 2 else 1 - par)
                    if not first or u >= 1:
                        pe.wait_ge(s["probs_done"], 2 * U)
                    scores(U, u, par, 1)
                    if n >= 1:
                        weigh_values(4 * hp + n - 1, n - 1, par, h, not first or n >= 3)
                    elif not first:
                        weigh_values(4 * hp + n - 1, NB - 1, 1 - par, h, True)

            loop_pairs(pe, body)
            weigh_values(4 * HP - 1, NB - 1, 1, 0, True)
            weigh_values(4 * HP - 1, NB - 1, 1, 1, True)

            pe.wait_ge(s["bias_prod"], 2)
            pe.wait_ge(s["psum_read"], 4 * HP - 1)
            for hp in range(HP):
                pe.matmul(outs[0][:, 0:P], ones[:, :], bvw[:, hp, :], start=(hp == 0), stop=False)
            pe.matmul(outs[0][:, 0:P], ones[0:1, :], bo_row[:, :], start=False, stop=True).then_inc(s["bias_sum"], 1)

            for t in range(NT):
                pe.wait_ge(s["oT_done"], 4 * (HP - 1) + t // QT + 1)
                cols = slice(t * P, (t + 1) * P)
                for hp in range(HP):
                    last = three(near[t // 4][:, (t % 4) * P:(t % 4 + 1) * P], oT_hi[:, hp, cols], oT_lo[:, hp, cols],
                                 wo_hi[:, hp, :], wo_lo[:, hp, :], start=(hp == 0), stop=(hp == HP - 1))
                if t % 4 == 3:
                    last.then_inc(s["y_done"], 1)
            for half in range(2):
                turn_x(half, 2 + half)
            pe.wait_ge(s["router_done"], 1)
            pe.wait_ge(s["xT_done"], 4)
            pe.wait_ge(s["attn_done"], 1)
            for t in range(NT):
                cols = slice(t * P, (t + 1) * P)
                last = three(near[0][:, 16 * t:16 * t + NE], xT_hi[:, cols], xT_lo[:, cols], router_hi[:, :], router_lo[:, :])
            last.then_inc(s["logits_done"], 1)

            def gate_up(e, C, c, par, first):
                tc, ft = c // 2, c % 2
                if c == 0:
                    pe.wait_ge(s["wf_done"], 2 * e + 1)
                if not first or c >= 2:
                    pe.wait_ge(s["hid_done"], C - 1)
                cols = slice(tc * 512, (tc + 1) * 512)
                g = slice(ft * P, (ft + 1) * P)
                u = slice((FT + ft) * P, (FT + ft + 1) * P)
                three(score[c % 2][:, :], wf_hi[:, par, g], wf_lo[:, par, g], xT_hi[:, cols], xT_lo[:, cols])
                three(outs[c % 2][:, :], wf_hi[:, par, u], wf_lo[:, par, u], xT_hi[:, cols],
                      xT_lo[:, cols]).then_inc(s["gu_done"], 1)

            def down(e, par, yb, first):
                if yb == 0:
                    pe.wait_ge(s["wf_done"], 2 * e + 2)
                pe.wait_ge(s["hid_lo_done"], 4 * e + 2 * yb + 2)
                if not first:
                    pe.wait_ge(s["summed"], 2 * e - 1 + yb)
                for t in range(4):
                    cols = slice((4 * yb + t) * P, (4 * yb + t + 1) * P)
                    for ft in range(FT):
                        d = slice((2 * FT + ft) * P, (2 * FT + ft + 1) * P)
                        last = three(misc[yb][:, t * P:(t + 1) * P], hid_hi[:, par, ft, cols], hid_lo[:, par, ft, cols],
                                     wf_hi[:, par, d], wf_lo[:, par, d], start=(ft == 0), stop=(ft == FT - 1))
                last.then_inc(s["down_done"], 1)

            def expert(e, par, first, last):
                second = not first and isinstance(e, int) and e == 1
                for c in range(4):
                    gate_up(e, 4 * e + c, c, par, first)
                    if c in (1, 2) and not first:
                        down(e - 1, 1 - par, c - 1, second)

            loop_experts(pe, expert)
            down(NE - 1, 0, 0, False)
            down(NE - 1, 0, 1, False)


def kernel(x, ctx_1024, g_xattn, g_ffn, L0_xattn_Wq, L0_xattn_bq, L0_xattn_Wk, L0_xattn_bk, L0_xattn_Wv,
           L0_xattn_bv, L0_xattn_Wo, L0_xattn_bo, L0_ffn_router_w, L0_ffn_w_gate, L0_ffn_w_up, L0_ffn_w_down,
           L0_ffn_sw_gate, L0_ffn_sw_up, L0_ffn_sw_down, L0_ffn_gate_w):
    import numpy as np
    import concourse.bacc as bacc
    from concourse import mybir as mb
    from concourse.bass_utils import run_bass_kernel_spmd

    a = np.asarray
    x, c = a(x), a(ctx_1024)
    B, Lq, Em = x.shape
    pairs = L0_xattn_Wq.shape[0] // 128
    gate = np.concatenate([a(L0_ffn_w_gate), a(L0_ffn_sw_gate)[None]])
    up = np.concatenate([a(L0_ffn_w_up), a(L0_ffn_sw_up)[None]])
    down = np.concatenate([a(L0_ffn_w_down), a(L0_ffn_sw_down)[None]])
    n_e, F, _ = down.shape
    down = down.reshape(n_e, F // 128, 128, Em).transpose(0, 2, 1, 3).reshape(n_e, 128, -1)
    wqkv = np.stack([a(w).reshape(pairs, 128, Em).transpose(2, 0, 1) for w in (L0_xattn_Wq, L0_xattn_Wk, L0_xattn_Wv)], axis=2)
    data = {
        "xs": x.reshape(B * Lq, Em),
        "ctxT": c.reshape(-1, Em).T,
        "g_xattn": np.broadcast_to(a(g_xattn).reshape(1, 1), (128, 1)),
        "g_ffn": np.broadcast_to(a(g_ffn).reshape(1, 1), (128, 1)),
        "wqkv": wqkv.reshape(Em, pairs, 3 * 128),
        "bqk": np.stack([a(L0_xattn_bq).reshape(pairs, 128).T, a(L0_xattn_bk).reshape(pairs, 128).T], axis=2),
        "bv": a(L0_xattn_bv).reshape(pairs, 128).T,
        "woT": a(L0_xattn_Wo).T,
        "bo": a(L0_xattn_bo).reshape(1, Em),
        "routerT": np.concatenate([a(L0_ffn_router_w), a(L0_ffn_gate_w)]).T,
        "wffn": np.concatenate([gate, up, down], axis=2),
    }
    nc = bacc.Bacc("TRN2", target_bir_lowering=False, num_devices=1)
    arrays, args = {}, {}
    for name, value in data.items():
        value = np.ascontiguousarray(value)
        arrays[name] = value
        args[name] = nc.dram_tensor(name, value.shape, mb.dt.from_np(value.dtype), kind="ExternalInput").ap()
    y = nc.dram_tensor("y", (B * Lq, Em), mb.dt.float32, kind="ExternalOutput").ap()
    flamingo_block(nc, out=y, **args)
    result = run_bass_kernel_spmd(nc, [arrays], core_ids=[0])
    return result.results[0]["y"].reshape(B, Lq, Em)
```

```python
from contextlib import ExitStack

import concourse.bass as bass
from concourse import mybir

P = 128
ALU = mybir.AluOpType
ACT = mybir.ActivationFunctionType
AX = mybir.AxisListType
F32 = mybir.dt.float32
F16 = mybir.dt.float16
BF16 = mybir.dt.bfloat16

ACT_SCALE = 4.0
W_SCALE = 16.0
PROJ_SCALE = ACT_SCALE * W_SCALE
ROW_SCALE = 2048.0
EPS = 1e-5
NEVER = 4.0


def flamingo_block(nc, xs, ctxT, g_xattn, g_ffn, wqkv, bqk, bv, woT, bo, routerT, wffn, out):
    T, E = xs.shape
    HP = wqkv.shape[1]
    NB = 4
    L = T // NB
    S = ctxT.shape[1] // NB
    D = 64
    NT = T // P
    KT = S // P
    QT = L // P
    NE = wffn.shape[0]
    NR = NE - 1
    FT = 2
    UN = 2 * NB
    EXP_SCALE = 1.0 / (8.0 * PROJ_SCALE * PROJ_SCALE)
    HALF = T // 2
    assert E == P and L == 256 and S == 512 and T == 1024 and HP == 8 and NE == 9

    with ExitStack() as ctx:
        def sb(name, shape, dt):
            return ctx.enter_context(nc.sbuf_tensor(name, shape, dt))

        def sem(name):
            return ctx.enter_context(nc.semaphore(name))

        x_in = sb("x_in", [P, NT, P], F32)
        x_norm = sb("x_norm", [P, NT, P], F32)
        x_mid = sb("x_mid", [P, NT, P], F32)
        xT_hi = sb("xT_hi", [P, T], F16)
        xT_lo = sb("xT_lo", [P, T], F16)
        ctx_hi = sb("ctx_hi", [P, NB * S], F16)
        ctx_lo = sb("ctx_lo", [P, NB * S], F16)
        w_qkv = sb("w_qkv", [P, HP, 3 * P], F32)
        w_hi = sb("w_hi", [P, 2, 3 * P], F16)
        w_lo = sb("w_lo", [P, 2, 3 * P], F16)
        wo = sb("wo", [P, HP, P], F32)
        wo_hi = sb("wo_hi", [P, HP, P], F16)
        wo_lo = sb("wo_lo", [P, HP, P], F16)
        bias_qk = sb("bias_qk", [P, HP, 2], F32)
        bias_pair = sb("bias_pair", [P, 2, 2], F32)
        bias_v = sb("bias_v", [P, HP], F32)
        bo_row = sb("bo_row", [1, P], F32)
        g_col = sb("g_col", [P, 2], F32)
        tanh_g = sb("tanh_g", [P, 2], F32)
        q_hi = sb("q_hi", [P, T], F16)
        q_lo = sb("q_lo", [P, T], F16)
        k_hi = sb("k_hi", [P, NB * S], F16)
        k_lo = sb("k_lo", [P, NB * S], F16)
        k_both = sb("k_both", [P, 2, 2, NB * S], F16)
        k_row = sb("k_row", [P, 2, 2, NB * S], F16)
        q_twice = sb("q_twice", [P, 2, 2, T], F16)
        q_row = sb("q_row", [P, 2, 2, T], F16)
        v_sb = sb("v_sb", [P, 2, NB * KT, P], F32)
        probs = sb("probs", [P, 4, KT * L], F32)
        part_sum = sb("part_sum", [P, 2 * L], F32)
        prob_sum = sb("prob_sum", [P, 4, L], F32)
        max_cols = sb("max_cols", [P, 2, QT, P], BF16)
        neg_ident = sb("neg_ident", [P, P], BF16)
        ident = sb("ident", [P, P], F32)
        ones = sb("ones", [P, P], F32)
        ln_den = sb("ln_den", [P, L], F32)
        rec_den = sb("rec_den", [P, L], F32)
        den_rec = sb("den_rec", [P, L], F32)
        o_rec = sb("o_rec", [P, L], F32)
        o_norm = sb("o_norm", [P, 2, L], F32)
        oT_hi = sb("oT_hi", [P, HP, T], F16)
        oT_lo = sb("oT_lo", [P, HP, T], F16)
        stats = sb("stats", [P, NT, 6], F32)
        mean_var = sb("mean_var", [P, NT, 2], F32)
        ln_var = sb("ln_var", [P, NT], F32)
        rstd0 = sb("rstd0", [P, NT], F32)
        newton = sb("newton", [P, NT], F32)
        newton2 = sb("newton2", [P, NT], F32)
        rstd = sb("rstd", [P, NT], F32)
        eps_col = sb("eps_col", [P, 1], F32)
        bias_out = sb("bias_out", [P, P], F32)
        attn = sb("attn", [P, 4 * P], F32)
        router = sb("router", [P, NE], F32)
        router_hi = sb("router_hi", [P, NE], F16)
        router_lo = sb("router_lo", [P, NE], F16)
        logits = sb("logits", [P, NT, NE], F32)
        r_a = sb("r_a", [P, NT, NR], F32)
        r_b = sb("r_b", [P, NT, NR], F32)
        r_c = sb("r_c", [P, NT, NR], F32)
        prob_e = sb("prob_e", [P, NT, NR], F32)
        first_e = sb("first_e", [P, NT, NR], F32)
        order_e = sb("order_e", [P, NR], F32)
        r_m = sb("r_m", [P, NT], F32)
        r_s = sb("r_s", [P, NT], F32)
        gate_e = sb("gate_e", [P, NT], F32)
        mix = sb("mix", [P, NT, NE], F32)
        wf = sb("wf", [P, 2, 768], F32)

        ctx32 = probs[:, 0:2, :].rearrange("p a b -> p (a b)")
        bvw = v_sb[:, 1, 0:HP, :]
        silu = probs[:, 0, :].rearrange("p (a b) -> p a b", a=2)
        hid = probs[:, 1, :].rearrange("p (a b) -> p a b", a=2)
        hid_hi = k_both[:, 0, :, :].rearrange("p a (f t) -> p a f t", f=FT)
        hid_lo = k_both[:, 1, :, :].rearrange("p a (f t) -> p a f t", f=FT)
        wf_hi = k_hi[:, 0:1536].rearrange("p (a b) -> p a b", a=2)
        wf_lo = k_lo[:, 0:1536].rearrange("p (a b) -> p a b", a=2)

        banks = [ctx.enter_context(nc.psum_tensor(f"bank{i}", [P, 512], F32)) for i in range(8)]
        near = [banks[0], banks[1]]
        score = [banks[2], banks[3]]
        outs = [banks[4], banks[5]]
        misc = [banks[6], banks[7]]

        names = """x0_loaded x1_loaded ctx0_loaded ctx1_loaded ctx2_loaded ctx3_loaded w_first_loaded
        w_rest_loaded small_loaded bias_loaded wo_loaded wf0_loaded wf1_loaded consts
        pool_step stats_done var_ready ln_half rstd_done normed transposed xT_hi_done xT_done
        ctx_hi_done ctx_done w_hi_done w_done bias_done wo_done bias_prod bias_sum bias_out_done
        projected hi_done lo_done v_done q_moved k_moved near_done max_done shift_made shift_done
        scores_done probs_done sums_half sums_done pv_done ln_done rec_done div_half psum_read div_done
        oT_hi_done oT_done y_done attn_half attn_done router_done logits_done route route_exp route_act
        mix_done wf_hi_done wf_done gu_done silu_done hid_done hid_hi_done hid_lo_done down_done
        summed stored tanh_done router_hi_done""".split()
        s = {n: sem(n) for n in names}
        block = ctx.enter_context(nc.Block())

        GROUP = {(1, 0): 0, (1, 1): 1, (2, 0): 2, (2, 1): 3, (3, 0): 4, (3, 1): 5, (4, 0): 6, (5, 0): 7,
                 (6, 0): 8, (7, 0): 9}

        def loop_pairs(eng, body):
            body(0, 0, True, False)
            with eng.Fori(0, (HP - 2) // 2) as i:
                body(2 * i + 1, 1, False, False)
                body(2 * i + 2, 0, False, False)
            body(HP - 1, 1, False, True)

        def loop_experts(eng, body):
            body(0, 0, True, False)
            body(1, 1, False, False)
            with eng.Fori(0, (NE - 3) // 2) as i:
                body(2 * i + 2, 0, False, False)
                body(2 * i + 3, 1, False, False)
            body(NE - 1, 0, False, True)

        @block.sync
        def _(sp):
            xv = xs.rearrange("(t p) e -> p t e", p=P)
            for h in range(2):
                sp.dma_start(x_in[:, 4 * h:4 * h + 4, :], xv[:, 4 * h:4 * h + 4, :]).then_inc(s[f"x{h}_loaded"], 16)
            sp.dma_start(w_qkv[:, 0:1, :], wqkv[:, 0:1, :]).then_inc(s["w_first_loaded"], 16)
            sp.dma_start(bias_qk[:, :, :], bqk).then_inc(s["bias_loaded"], 16)
            for n in range(NB):
                sp.dma_start(ctx32[:, n * S:(n + 1) * S], ctxT[:, n * S:(n + 1) * S]).then_inc(s[f"ctx{n}_loaded"], 16)
            sp.dma_start(w_qkv[:, 1:HP, :], wqkv[:, 1:HP, :]).then_inc(s["w_rest_loaded"], 16)
            sp.dma_start(wo[:, :, :], woT.rearrange("(h p) e -> p h e", p=P)).then_inc(s["wo_loaded"], 16)
            for t, src in ((bias_v[:, :], bv), (router[:, :], routerT), (bo_row[:, :], bo),
                           (g_col[:, 0:1], g_xattn), (g_col[:, 1:2], g_ffn)):
                sp.dma_start(t, src).then_inc(s["small_loaded"], 16)
            for e in range(2):
                sp.dma_start(wf[:, e, :], wffn[e]).then_inc(s[f"wf{e}_loaded"], 16)

            def move(hp1, par1, first):
                sp.wait_ge(s["lo_done"], 6 * hp1 + 2)
                if not first:
                    sp.wait_ge(s["scores_done"], 16 * hp1 - 16)
                for h in range(2):
                    rows = slice(D * h, D * h + D)
                    sp.dma_start(q_twice[0:D, par1, h, :], q_hi[rows, :]).then_inc(s["q_moved"], 16)
                    sp.dma_start(q_twice[D:P, par1, h, :], q_hi[rows, :]).then_inc(s["q_moved"], 16)
                    sp.dma_start(q_row[0:D, par1, h, :], q_lo[rows, :]).then_inc(s["q_moved"], 16)
                sp.wait_ge(s["lo_done"], 6 * hp1 + 6)
                for h in range(2):
                    rows = slice(D * h, D * h + D)
                    sp.dma_start(k_both[0:D, par1, h, :], k_hi[rows, :]).then_inc(s["k_moved"], 16)
                    sp.dma_start(k_both[D:P, par1, h, :], k_lo[rows, :]).then_inc(s["k_moved"], 16)
                    sp.dma_start(k_row[0:D, par1, h, :], k_hi[rows, :]).then_inc(s["k_moved"], 16)

            move(0, 0, True)
            move(1, 1, True)
            with sp.Fori(0, (HP - 2) // 2) as i:
                move(2 * i + 2, 0, False)
                move(2 * i + 3, 1, False)

            def load_expert(e, par):
                sp.wait_ge(s["wf_done"], 2 * e - 2)
                sp.dma_start(wf[:, par:par + 1, :], wffn[bass.ds(e, 1)].rearrange("e p f -> p e f")).then_inc(s[f"wf{par}_loaded"], 16)

            with sp.Fori(0, 3) as i:
                load_expert(2 * i + 2, 0)
                load_expert(2 * i + 3, 1)
            load_expert(NE - 1, 0)

            ov = out.rearrange("(t p) e -> p t e", p=P)
            for h in range(2):
                sp.wait_ge(s["summed"], 2 * NE - 1 + h)
                sp.dma_start(ov[:, 4 * h:4 * h + 4, :], x_mid[:, 4 * h:4 * h + 4, :]).then_inc(s["stored"], 16)
            sp.wait_ge(s["stored"], 32)

        @block.gpsimd
        def _(pool):
            pool.memset(ident[:, :], 0.0).then_inc(s["pool_step"], 1)
            pool.memset(neg_ident[:, :], 0.0).then_inc(s["pool_step"], 1)
            pool.wait_ge(s["pool_step"], 2)
            pool.affine_select(out=ident[:, :], in_=ident[:, :], compare_op=ALU.not_equal, fill=1.0, base=0,
                               pattern=[[-1, P]], channel_multiplier=1).then_inc(s["consts"], 1)
            pool.affine_select(out=neg_ident[:, :], in_=neg_ident[:, :], compare_op=ALU.not_equal,
                               fill=-1.0 / ROW_SCALE, base=0, pattern=[[-1, P]], channel_multiplier=1).then_inc(s["consts"], 1)
            pool.memset(max_cols[:, :, :, :], 0.0).then_inc(s["consts"], 1)
            pool.memset(ones[:, :], 1.0).then_inc(s["consts"], 1)
            for par in range(2):
                pool.wait_ge(s["consts"], 4 + 2 * par)
                pool.memset(q_row[D:P, par, :, :].bitcast(F32), 0.0).then_inc(s["consts"], 1)
                pool.wait_ge(s["consts"], 5 + 2 * par)
                pool.memset(k_row[D:P, par, :, :].bitcast(F32), 0.0).then_inc(s["pool_step"], 1)
                pool.wait_ge(s["pool_step"], 3 + par)
                pool.memset(k_row[D:D + 1, par, :, :], ROW_SCALE).then_inc(s["consts"], 1)
            pool.wait_ge(s["consts"], 8)
            for e in range(NR):
                last = pool.memset(order_e[:, e:e + 1], float(NR - e))
            last.then_inc(s["consts"], 1)
            pool.wait_ge(s["wo_loaded"], 16)
            pool.tensor_scalar(wo[:, :, :], wo[:, :, :], W_SCALE, None, ALU.mult).then_inc(s["wo_done"], 1)
            pool.wait_ge(s["wo_done"], 1)
            pool.tensor_scalar(wo_hi[:, :, :], wo[:, :, :], 1.0, None, ALU.mult).then_inc(s["wo_done"], 1)
            pool.wait_ge(s["wo_done"], 2)
            pool.tensor_tensor(wo_lo[:, :, :], wo[:, :, :], wo_hi[:, :, :], ALU.subtract).then_inc(s["wo_done"], 1)

            def low_o(m, hp, n):
                pool.wait_ge(s["oT_hi_done"], m + 1)
                pool.tensor_tensor(oT_lo[:, bass.ds(hp, 1), n * L:(n + 1) * L], o_norm[:, n % 2:n % 2 + 1, :],
                                   oT_hi[:, bass.ds(hp, 1), n * L:(n + 1) * L], ALU.subtract).then_inc(s["oT_done"], 1)

            def body(hp, par, first, last):
                for u in range(UN):
                    U, n, slot = hp * UN + u, u // 2, (u // 2) % 2 * 2 + u % 2
                    if not first or u >= 1:
                        pool.wait_ge(s["sums_done"], U)
                    pool.wait_ge(s["probs_done"], 2 * U + 2)
                    pool.tensor_tensor(part_sum[:, :], probs[:, slot, 0:2 * L], probs[:, slot, 2 * L:4 * L],
                                       ALU.add).then_inc(s["sums_half"], 1)
                    pool.wait_ge(s["sums_half"], U + 1)
                    pool.tensor_tensor(prob_sum[:, slot, :], part_sum[:, 0:L], part_sum[:, L:2 * L],
                                       ALU.add).then_inc(s["sums_done"], 1)
                    if u % 2 == 1:
                        if n >= 2:
                            low_o(4 * hp + n - 2, hp, n - 2)
                        elif not first:
                            low_o(4 * hp + n - 2, hp - 1, n + 2)

            loop_pairs(pool, body)
            low_o(4 * HP - 2, HP - 1, 2)
            low_o(4 * HP - 1, HP - 1, 3)

            def expert(e, par, first, last):
                for c in range(4):
                    C, tc, ft = 4 * e + c, c // 2, c % 2
                    pool.wait_ge(s["hid_hi_done"], C + 1)
                    pool.tensor_tensor(hid_lo[:, par, ft, tc * 512:(tc + 1) * 512], hid[:, c % 2, :],
                                       hid_hi[:, par, ft, tc * 512:(tc + 1) * 512], ALU.subtract).then_inc(s["hid_lo_done"], 1)

            loop_experts(pool, expert)

        @block.scalar
        def _(act):
            act.preload_act_table_set("natural_log_exp_and_others")

            def split_w(hp, par):
                act.activation(w_hi[:, par:par + 1, :], w_qkv[:, bass.ds(hp, 1), :], ACT.Copy,
                               scale=W_SCALE).then_inc(s["w_hi_done"], 1)

            def rstd_guess(half, at):
                act.wait_ge(s["stats_done"], at + 1)
                act.activation(ln_var[:, 4 * half:4 * half + 4], mean_var[:, 4 * half:4 * half + 4, 1], ACT.Ln,
                               bias=eps_col[:, 0:1]).then_inc(s["ln_half"], 1)
                act.wait_ge(s["ln_half"], at + 1)
                act.activation(rstd0[:, 4 * half:4 * half + 4], ln_var[:, 4 * half:4 * half + 4], ACT.Exp,
                               scale=-0.5).then_inc(s["var_ready"], 1)

            def high_x(half, at):
                act.wait_ge(s["transposed"], at + 1)
                act.activation(xT_hi[:, half * HALF:(half + 1) * HALF], misc[half][:, :], ACT.Copy).then_inc(s["xT_hi_done"], 1)

            rstd_guess(0, 0)
            act.wait_ge(s["w_first_loaded"], 16)
            split_w(0, 0)
            rstd_guess(1, 1)
            for n in range(NB):
                act.wait_ge(s[f"ctx{n}_loaded"], 16)
                act.activation(ctx_hi[:, n * S:(n + 1) * S], ctx32[:, n * S:(n + 1) * S], ACT.Copy,
                               scale=ACT_SCALE).then_inc(s["ctx_hi_done"], 1)
                if n < 2:
                    high_x(n, n)

            def evacuate(hp1, par1, g, first):
                act.wait_ge(s["projected"], 10 * hp1 + g + 1)
                if g == 0:
                    act.wait_ge(s["bias_done"], hp1 + 1)
                if g < 2:
                    if g == 0 and not first:
                        act.wait_ge(s["q_moved"], 96 * hp1)
                    act.activation(q_hi[:, g * 512:(g + 1) * 512], misc[g % 2][:, :], ACT.Identity,
                                   bias=bias_pair[:, par1, 0:1]).then_inc(s["hi_done"], 1)
                elif g < 6:
                    if g == 2 and not first:
                        act.wait_ge(s["k_moved"], 96 * hp1)
                    act.activation(k_hi[:, (g - 2) * 512:(g - 1) * 512], misc[g % 2][:, :], ACT.Identity,
                                   bias=bias_pair[:, par1, 1:2]).then_inc(s["hi_done"], 1)
                else:
                    act.activation(v_sb[:, par1, (g - 6) * KT:(g - 5) * KT, :], misc[g % 2][:, :].rearrange("p (a b) -> p a b", a=KT),
                                   ACT.Copy).then_inc(s["v_done"], 1)

            def place_shift(U, u, par, qt):
                act.wait_ge(s["shift_made"], 2 * U + qt + 1)
                at = u // 2 * L + qt * P
                act.activation(q_row[D:D + 1, par, u % 2, at:at + P], near[qt][D:D + 1, 0:P],
                               ACT.Copy).then_inc(s["shift_done"], 1)

            def reciprocal_guess(m, n, first=False):
                if not first:
                    act.wait_ge(s["psum_read"], m)
                act.wait_ge(s["pv_done"], m + 1)
                act.activation(ln_den[:, :], outs[n % 2][:, L:2 * L], ACT.Ln).then_inc(s["ln_done"], 1)
                act.wait_ge(s["ln_done"], m + 1)
                act.activation(rec_den[:, :], ln_den[:, :], ACT.Exp, scale=-1.0).then_inc(s["rec_done"], 1)

            def high_o(m, hp, n):
                act.wait_ge(s["div_done"], m + 1)
                act.activation(oT_hi[:, bass.ds(hp, 1), n * L:(n + 1) * L], o_norm[:, n % 2:n % 2 + 1, :],
                               ACT.Copy).then_inc(s["oT_hi_done"], 1)

            for g in range(10):
                evacuate(0, 0, g, True)
            act.wait_ge(s["consts"], 5)
            place_shift(0, 0, 0, 0)
            place_shift(0, 0, 0, 1)

            def body(hp, par, first, last):
                for u in range(UN):
                    U, n, h = hp * UN + u, u // 2, u % 2
                    slot = n % 2 * 2 + h
                    if u == UN - 1 and first:
                        act.wait_ge(s["consts"], 7)
                    if u == 0 and not last:
                        if first:
                            act.wait_ge(s["w_rest_loaded"], 16)
                        split_w(hp + 1, 1 - par)
                    for half in range(2):
                        if u < UN - 1:
                            place_shift(U + 1, u + 1, par, half)
                        elif not last:
                            place_shift(U + 1, 0, 1 - par, half)
                        act.wait_ge(s["scores_done"], 2 * U + half + 1)
                        if half == 0 and (not first or n >= 2):
                            act.wait_ge(s["pv_done"], 4 * hp + n - 1)
                        act.activation(probs[:, slot, half * 512:(half + 1) * 512], score[half][:, :], ACT.Exp,
                                       scale=EXP_SCALE).then_inc(s["probs_done"], 1)
                        if not last and (u, half) in GROUP:
                            evacuate(hp + 1, 1 - par, GROUP[u, half], False)
                        if not first or n >= 2:
                            if (h, half) == (0, 0):
                                reciprocal_guess(4 * hp + n - 2, n % 2, first and n == 2)
                        if (h, half) == (0, 1):
                            if n >= 3:
                                high_o(4 * hp + n - 3, hp, n - 3)
                            elif not first:
                                high_o(4 * hp + n - 3, hp - 1, n + 1)

            loop_pairs(act, body)
            reciprocal_guess(4 * HP - 2, 0)
            high_o(4 * HP - 3, HP - 1, 1)
            high_o(4 * HP - 2, HP - 1, 2)
            reciprocal_guess(4 * HP - 1, 1)
            high_o(4 * HP - 1, HP - 1, 3)

            act.wait_ge(s["small_loaded"], 80)
            act.activation(tanh_g[:, :], g_col[:, :], ACT.Exp, scale=2.0).then_inc(s["tanh_done"], 1)
            act.activation(router_hi[:, :], router[:, :], ACT.Copy, scale=W_SCALE).then_inc(s["router_hi_done"], 1)
            for half in range(2):
                rstd_guess(half, 2 + half)
            for half in range(2):
                high_x(half, 2 + half)

            act.wait_ge(s["route_exp"], 1)
            act.activation(r_b[:, :, :], r_a[:, :, :], ACT.Exp).then_inc(s["route_act"], 1)
            act.activation(gate_e[:, :], logits[:, :, NR], ACT.Exp, scale=-1.0).then_inc(s["route_act"], 1)

            def split_gate_up(e, par):
                act.wait_ge(s[f"wf{par}_loaded"], 8 * (e - par) + 16)
                act.activation(wf_hi[:, par, 0:512], wf[:, par, 0:512], ACT.Copy, scale=W_SCALE).then_inc(s["wf_hi_done"], 1)

            def split_down(par):
                act.activation(wf_hi[:, par, 512:768], wf[:, par, 512:768], ACT.Copy, scale=W_SCALE).then_inc(s["wf_hi_done"], 1)

            split_gate_up(0, 0)
            split_down(0)

            def high_hidden(C, par, c):
                act.wait_ge(s["hid_done"], C + 1)
                act.activation(hid_hi[:, par, c % 2, (c // 2) * 512:(c // 2 + 1) * 512], hid[:, c % 2, :],
                               ACT.Copy).then_inc(s["hid_hi_done"], 1)

            def expert(e, par, first, last):
                for c in range(4):
                    C = 4 * e + c
                    act.wait_ge(s["gu_done"], C + 1)
                    if not first or c >= 2:
                        act.wait_ge(s["hid_done"], C - 1)
                    act.activation(silu[:, c % 2, :], score[c % 2][:, :], ACT.Silu, scale=1.0 / PROJ_SCALE).then_inc(s["silu_done"], 1)
                    if c == 0:
                        if not first:
                            high_hidden(C - 1, 1 - par, 3)
                    else:
                        if c == 1 and not first:
                            act.wait_ge(s["down_done"], 2 * e - 2)
                        high_hidden(C - 1, par, c - 1)
                    if c == 1 and not last:
                        split_gate_up(e + 1, 1 - par)
                    if c == 3 and not last:
                        if not first:
                            act.wait_ge(s["down_done"], 2 * e)
                        split_down(1 - par)

            loop_experts(act, expert)
            high_hidden(4 * NE - 1, 0, 3)

        @block.vector
        def _(dve):
            dve.memset(eps_col[:, :], EPS)

            def layer_stats(src, half, at):
                for t in range(4 * half, 4 * half + 4):
                    dve.bn_stats(stats[:, t, :], src[:, t, :]).then_inc(s["attn_half"], 1)
                for j, t in enumerate(range(4 * half, 4 * half + 4)):
                    dve.wait_ge(s["attn_half"], 4 * at + j + 1)
                    last = dve.bn_aggr(mean_var[:, t, :], stats[:, t, :])
                last.then_inc(s["stats_done"], 1)

            def layer_norm(src, half, at):
                hs = slice(4 * half, 4 * half + 4)
                step = 4 * at
                dve.wait_ge(s["var_ready"], at + 1)
                dve.wait_ge(s["stats_done"], at + 1)
                dve.scalar_tensor_tensor(newton[:, hs], mean_var[:, hs, 1], EPS, rstd0[:, hs], ALU.add,
                                         ALU.mult).then_inc(s["rstd_done"], 1)
                dve.wait_ge(s["rstd_done"], step + 1)
                dve.tensor_tensor(newton2[:, hs], newton[:, hs], rstd0[:, hs], ALU.mult).then_inc(s["rstd_done"], 1)
                dve.wait_ge(s["rstd_done"], step + 2)
                dve.tensor_scalar(newton[:, hs], newton2[:, hs], -0.5 * ACT_SCALE, 1.5 * ACT_SCALE, ALU.mult,
                                  ALU.add).then_inc(s["rstd_done"], 1)
                dve.wait_ge(s["rstd_done"], step + 3)
                dve.tensor_tensor(rstd[:, hs], newton[:, hs], rstd0[:, hs], ALU.mult).then_inc(s["rstd_done"], 1)
                dve.wait_ge(s["rstd_done"], step + 4)
                for t in range(4 * half, 4 * half + 4):
                    last = dve.tensor_scalar(x_norm[:, t, :], src[:, t, :], mean_var[:, t, 0:1], rstd[:, t:t + 1],
                                             ALU.subtract, ALU.mult)
                last.then_inc(s["normed"], 1)

            def low_x(half, at):
                dve.wait_ge(s["xT_hi_done"], at + 1)
                dve.tensor_tensor(xT_lo[:, half * HALF:(half + 1) * HALF], misc[half][:, :],
                                  xT_hi[:, half * HALF:(half + 1) * HALF], ALU.subtract).then_inc(s["xT_done"], 1)

            def low_w(hp, par):
                dve.tensor_scalar(bias_pair[:, par:par + 1, :], bias_qk[:, bass.ds(hp, 1), :], PROJ_SCALE, None,
                                  ALU.mult).then_inc(s["bias_done"], 1)
                dve.wait_ge(s["w_hi_done"], hp + 1)
                dve.scalar_tensor_tensor(w_lo[:, par:par + 1, :], w_qkv[:, bass.ds(hp, 1), :], W_SCALE,
                                         w_hi[:, par:par + 1, :], ALU.mult, ALU.subtract).then_inc(s["w_done"], 1)

            for half in range(2):
                dve.wait_ge(s[f"x{half}_loaded"], 16)
                layer_stats(x_in, half, half)
            layer_norm(x_in, 0, 0)
            dve.wait_ge(s["bias_loaded"], 16)
            low_w(0, 0)
            layer_norm(x_in, 1, 1)
            for n in range(NB):
                dve.wait_ge(s["ctx_hi_done"], n + 1)
                dve.scalar_tensor_tensor(ctx_lo[:, n * S:(n + 1) * S], ctx32[:, n * S:(n + 1) * S], ACT_SCALE,
                                         ctx_hi[:, n * S:(n + 1) * S], ALU.mult, ALU.subtract).then_inc(s["ctx_done"], 1)
                if n < 2:
                    low_x(n, n)

            def low_part(hp1, par1, g):
                dve.wait_ge(s["hi_done"], 6 * hp1 + g + 1)
                if g == 0:
                    dve.wait_ge(s["bias_done"], hp1 + 1)
                if g < 2:
                    lo, hi, b, at = q_lo, q_hi, bias_pair[:, par1, 0:1], g * 512
                else:
                    lo, hi, b, at = k_lo, k_hi, bias_pair[:, par1, 1:2], (g - 2) * 512
                dve.scalar_tensor_tensor(lo[:, at:at + 512], misc[g % 2][:, :], b, hi[:, at:at + 512],
                                         ALU.add, ALU.subtract).then_inc(s["lo_done"], 1)

            def take_max(U, u, qt, first):
                dve.wait_ge(s["near_done"], 2 * U + qt + 1)
                if not first:
                    dve.wait_ge(s["shift_made"], 2 * U + qt - 3)
                dve.tensor_reduce(max_cols[:, u % 2, qt, D:D + 1], near[qt][:, :], AX.X, ALU.max).then_inc(s["max_done"], 1)

            def divide(m, n, first=False):
                if not first:
                    dve.wait_ge(s["div_done"], m)
                dve.wait_ge(s["rec_done"], m + 1)
                dve.tensor_tensor(den_rec[:, :], outs[n % 2][:, L:2 * L], rec_den[:, :], ALU.mult).then_inc(s["div_half"], 1)
                dve.tensor_tensor(o_rec[:, :], outs[n % 2][:, 0:L], rec_den[:, :], ALU.mult).then_inc(s["psum_read"], 1)
                dve.wait_ge(s["div_half"], m + 1)
                dve.wait_ge(s["psum_read"], m + 1)
                dve.scalar_tensor_tensor(o_norm[:, n % 2, :], den_rec[:, :], -2.0, o_rec[:, :], ALU.add,
                                         ALU.mult).then_inc(s["div_done"], 1)

            for g in range(6):
                low_part(0, 0, g)
            dve.wait_ge(s["small_loaded"], 80)
            dve.wait_ge(s["wo_done"], 3)
            dve.tensor_tensor(bvw, wo[:, :, :], bias_v[:, :].unsqueeze(2).broadcast_to([P, HP, P]), ALU.mult).then_inc(s["bias_prod"], 1)
            dve.tensor_scalar(bo_row[:, :], bo_row[:, :], W_SCALE, None, ALU.mult).then_inc(s["bias_prod"], 1)
            dve.wait_ge(s["consts"], 4)
            for i in range(4):
                take_max(i // 2, i // 2, i % 2, True)
            dve.wait_ge(s["bias_sum"], 1)
            dve.tensor_scalar(bias_out[:, :], outs[0][:, 0:P], 1.0 / W_SCALE, None, ALU.mult).then_inc(s["bias_out_done"], 1)

            def body(hp, par, first, last):
                for u in range(UN):
                    U, n, h = hp * UN + u, u // 2, u % 2
                    if u == 0 and not last:
                        low_w(hp + 1, 1 - par)
                    for half in range(2):
                        if not last and GROUP.get((u, half), 9) < 6:
                            low_part(hp + 1, 1 - par, GROUP[u, half])
                        if not (last and u >= UN - 2):
                            take_max(U + 2, u, half, False)
                        if (h, half) == (1, 0) and (not first or n >= 2):
                            if not first:
                                dve.wait_ge(s["oT_done"], 4 * hp + n - 3)
                            divide(4 * hp + n - 2, n % 2, first and n == 2)

            loop_pairs(dve, body)
            dve.wait_ge(s["oT_done"], 4 * HP - 3)
            divide(4 * HP - 2, 0)
            dve.wait_ge(s["oT_done"], 4 * HP - 2)
            divide(4 * HP - 1, 1)

            dve.wait_ge(s["bias_out_done"], 1)
            dve.wait_ge(s["tanh_done"], 1)
            dve.tensor_scalar(tanh_g[:, :], tanh_g[:, :], 1.0, None, ALU.add).then_inc(s["tanh_done"], 1)
            dve.wait_ge(s["tanh_done"], 2)
            dve.reciprocal(tanh_g[:, :], tanh_g[:, :]).then_inc(s["tanh_done"], 1)
            dve.wait_ge(s["tanh_done"], 3)
            dve.tensor_scalar(tanh_g[:, :], tanh_g[:, :], -2.0, 1.0, ALU.mult, ALU.add).then_inc(s["tanh_done"], 1)
            dve.wait_ge(s["tanh_done"], 4)
            for half in range(2):
                hs = slice(4 * half, 4 * half + 4)
                dve.wait_ge(s["y_done"], half + 1)
                if half:
                    dve.wait_ge(s["attn_done"], half)
                dve.scalar_tensor_tensor(attn[:, :].rearrange("p (a b) -> p a b", a=4), near[half][:, :].rearrange("p (a b) -> p a b", a=4),
                                         -1.0 / (PROJ_SCALE * W_SCALE), bias_out[:, :].unsqueeze(1).broadcast_to([P, 4, P]),
                                         ALU.mult, ALU.add).then_inc(s["route"], 1)
                dve.wait_ge(s["route"], half + 1)
                dve.scalar_tensor_tensor(x_mid[:, hs, :].rearrange("p a b -> p (a b)"), attn[:, :], tanh_g[:, 0:1],
                                         x_in[:, hs, :].rearrange("p a b -> p (a b)"), ALU.mult, ALU.add).then_inc(s["attn_done"], 1)
                dve.wait_ge(s["attn_done"], half + 1)
                layer_stats(x_mid, half, 2 + half)
            for half in range(2):
                layer_norm(x_mid, half, 2 + half)
            dve.wait_ge(s["router_hi_done"], 1)
            dve.scalar_tensor_tensor(router_lo[:, :], router[:, :], W_SCALE, router_hi[:, :], ALU.mult,
                                     ALU.subtract).then_inc(s["router_done"], 1)
            for half in range(2):
                low_x(half, 2 + half)

            def low_gate_up(e, par):
                dve.wait_ge(s["wf_hi_done"], 2 * e + 1)
                dve.scalar_tensor_tensor(wf_lo[:, par, 0:512], wf[:, par, 0:512], W_SCALE, wf_hi[:, par, 0:512],
                                         ALU.mult, ALU.subtract).then_inc(s["wf_done"], 1)

            def low_down(e, par):
                dve.wait_ge(s["wf_hi_done"], 2 * e + 2)
                dve.scalar_tensor_tensor(wf_lo[:, par, 512:768], wf[:, par, 512:768], W_SCALE, wf_hi[:, par, 512:768],
                                         ALU.mult, ALU.subtract).then_inc(s["wf_done"], 1)

            count = [2]

            def link(ins):
                count[0] += 1
                ins.then_inc(s["route"], 1)
                dve.wait_ge(s["route"], count[0])

            def over_experts(col):
                return col[:, :].unsqueeze(2).broadcast_to([P, NT, NR])

            order = order_e[:, :].unsqueeze(1).broadcast_to([P, NT, NR])
            dve.wait_ge(s["logits_done"], 1)
            link(dve.tensor_scalar(logits[:, :, :], banks[0][:, 0:16 * NT].rearrange("p (t e) -> p t e", e=16)[:, :, 0:NE],
                                   1.0 / PROJ_SCALE, None, ALU.mult))
            link(dve.tensor_reduce(r_m[:, :], logits[:, :, 0:NR], AX.X, ALU.max))
            dve.tensor_tensor(r_a[:, :, :], logits[:, :, 0:NR], over_experts(r_m), ALU.subtract).then_inc(s["route_exp"], 1)
            low_gate_up(0, 0)
            low_down(0, 0)
            dve.wait_ge(s["route_act"], 2)
            link(dve.tensor_reduce(r_s[:, :], r_b[:, :, :], AX.X, ALU.add))
            link(dve.reciprocal(r_m[:, :], r_s[:, :]))
            link(dve.tensor_tensor(prob_e[:, :, :], r_b[:, :, :], over_experts(r_m), ALU.mult))
            dve.wait_ge(s["consts"], 9)

            def pick(dst, src):
                link(dve.tensor_reduce(r_m[:, :], src[:, :, :], AX.X, ALU.max))
                link(dve.tensor_tensor(r_a[:, :, :], src[:, :, :], over_experts(r_m), ALU.is_ge))
                link(dve.tensor_tensor(r_b[:, :, :], r_a[:, :, :], order, ALU.mult))
                link(dve.tensor_reduce(r_s[:, :], r_b[:, :, :], AX.X, ALU.max))
                link(dve.tensor_tensor(dst[:, :, :], r_b[:, :, :], over_experts(r_s), ALU.is_equal))

            pick(first_e, prob_e)
            link(dve.scalar_tensor_tensor(r_c[:, :, :], first_e[:, :, :], -NEVER, prob_e[:, :, :], ALU.mult, ALU.add))
            pick(r_a, r_c)
            link(dve.tensor_tensor(r_b[:, :, :], r_a[:, :, :], first_e[:, :, :], ALU.add))
            link(dve.tensor_tensor(mix[:, :, 0:NR], r_b[:, :, :], prob_e[:, :, :], ALU.mult))
            link(dve.tensor_scalar(r_s[:, :], gate_e[:, :], 1.0, None, ALU.add))
            link(dve.reciprocal(mix[:, :, NR], r_s[:, :]))
            dve.tensor_scalar(mix[:, :, :], mix[:, :, :], tanh_g[:, 1:2], 1.0 / (PROJ_SCALE * W_SCALE), ALU.mult,
                              ALU.mult).then_inc(s["mix_done"], 1)
            dve.wait_ge(s["mix_done"], 1)

            def combine(at, e, yb):
                dve.wait_ge(s["down_done"], at + 1)
                for t in range(4):
                    last = dve.scalar_tensor_tensor(x_mid[:, 4 * yb + t, :], misc[yb][:, t * P:(t + 1) * P],
                                                    mix[:, 4 * yb + t, bass.ds(e, 1)], x_mid[:, 4 * yb + t, :],
                                                    ALU.mult, ALU.add)
                last.then_inc(s["summed"], 1)

            def expert(e, par, first, last):
                for c in range(4):
                    C = 4 * e + c
                    dve.wait_ge(s["silu_done"], C + 1)
                    if not first or c >= 2:
                        dve.wait_ge(s["hid_lo_done"], C - 1)
                    dve.tensor_tensor(hid[:, c % 2, :], outs[c % 2][:, :], silu[:, c % 2, :], ALU.mult).then_inc(s["hid_done"], 1)
                    if not first and c >= 2:
                        combine(2 * e - 2 + c - 2, e - 1, c - 2)
                    if c == 1 and not last:
                        low_gate_up(e + 1, 1 - par)
                    if c == 3 and not last:
                        low_down(e + 1, 1 - par)

            loop_experts(dve, expert)
            combine(2 * NE - 2, NE - 1, 0)
            combine(2 * NE - 1, NE - 1, 1)

        @block.tensor
        def _(pe):
            def three(out_ap, lhs_hi, lhs_lo, rhs_hi, rhs_lo, start=True, stop=True):
                pe.matmul(out_ap, lhs_hi, rhs_hi, start=start, stop=False)
                pe.matmul(out_ap, lhs_hi, rhs_lo, start=False, stop=False)
                return pe.matmul(out_ap, lhs_lo, rhs_hi, start=False, stop=stop)

            def turn_x(half, at):
                pe.wait_ge(s["normed"], at + 1)
                for j in range(4):
                    last = pe.transpose(misc[half][:, j * P:(j + 1) * P], x_norm[:, 4 * half + j, :], ident[:, :])
                last.then_inc(s["transposed"], 1)

            def project(hp1, par1, g, first):
                if g == 0:
                    pe.wait_ge(s["w_done"], hp1 + 1)
                if g >= 8:
                    pe.wait_ge(s["v_done"], 4 * hp1 + g - 7)
                elif g >= 2:
                    pe.wait_ge(s["lo_done"], 6 * hp1 + g - 1)
                elif not first:
                    pe.wait_ge(s["v_done"], 4 * hp1 + g - 1)
                out_ap = misc[g % 2]
                if g < 2:
                    cols = slice(g * 512, (g + 1) * 512)
                    last = three(out_ap[:, :], w_hi[:, par1, 0:P], w_lo[:, par1, 0:P], xT_hi[:, cols], xT_lo[:, cols])
                elif g < 6:
                    if first:
                        pe.wait_ge(s["ctx_done"], g - 1)
                    cols = slice((g - 2) * 512, (g - 1) * 512)
                    last = three(out_ap[:, :], w_hi[:, par1, P:2 * P], w_lo[:, par1, P:2 * P], ctx_hi[:, cols], ctx_lo[:, cols])
                else:
                    for kt in range(KT):
                        cols = slice(((g - 6) * KT + kt) * P, ((g - 6) * KT + kt + 1) * P)
                        last = three(out_ap[:, kt * P:(kt + 1) * P], ctx_hi[:, cols], ctx_lo[:, cols],
                                     w_hi[:, par1, 2 * P:3 * P], w_lo[:, par1, 2 * P:3 * P])
                last.then_inc(s["projected"], 1)

            def near_scores(u, par, qt):
                n, h = u // 2, u % 2
                cols = slice(n * L + qt * P, n * L + (qt + 1) * P)
                pe.matmul(near[qt][:, :], q_twice[:, par, h, cols], k_both[:, par, h, n * S:(n + 1) * S],
                          start=True, stop=True).then_inc(s["near_done"], 1)

            def turn_max(U, u, qt):
                pe.wait_ge(s["max_done"], 2 * U + qt + 1)
                pe.matmul(near[qt][:, 0:P], max_cols[:, u % 2, qt, :], neg_ident[:, :], start=True,
                          stop=True).then_inc(s["shift_made"], 1)

            def scores(U, u, par, half):
                n, h = u // 2, u % 2
                qs = slice(n * L, (n + 1) * L)
                for j in range(2):
                    kt = 2 * half + j
                    ks = slice(n * S + kt * P, n * S + (kt + 1) * P)
                    pe.matmul(score[half][:, j * L:(j + 1) * L], k_both[:, par, h, ks], q_twice[:, par, h, qs],
                              start=True, stop=False)
                    last = pe.matmul(score[half][:, j * L:(j + 1) * L], k_row[:, par, h, ks], q_row[:, par, h, qs],
                                     start=False, stop=True)
                last.then_inc(s["scores_done"], 1)

            def weigh_values(m, n, vpar, kt, guard):
                bank = outs[n % 2]
                if kt == 0:
                    pe.wait_ge(s["probs_done"], 4 * m + 4)
                    pe.wait_ge(s["v_done"], m + 1)
                    if guard:
                        pe.wait_ge(s["psum_read"], m - 1)
                for h in range(2):
                    pe.matmul(bank[D * h:D * h + D, 0:L], v_sb[:, vpar, n * KT + kt, D * h:D * h + D],
                              probs[:, n % 2 * 2 + h, kt * L:(kt + 1) * L], start=(kt == 0), stop=(kt == 3))
                if kt == 3:
                    pe.wait_ge(s["sums_done"], 2 * m + 2)
                    for h in range(2):
                        last = pe.matmul(bank[D * h:D * h + D, L:2 * L], ones[:, 0:D], prob_sum[:, n % 2 * 2 + h, :],
                                         start=True, stop=True)
                    last.then_inc(s["pv_done"], 1)

            pe.wait_ge(s["consts"], 1)
            for half in range(2):
                turn_x(half, half)
            pe.wait_ge(s["xT_done"], 2)
            for g in range(10):
                project(0, 0, g, True)
            pe.wait_ge(s["consts"], 6)
            pe.wait_ge(s["q_moved"], 96)
            pe.wait_ge(s["k_moved"], 96)
            for qt in range(QT):
                near_scores(0, 0, qt)
            for qt in range(QT):
                turn_max(0, 0, qt)
                pe.wait_ge(s["shift_done"], qt + 1)
                near_scores(1, 0, qt)
            turn_max(1, 1, 0)

            def body(hp, par, first, last):
                for u in range(UN):
                    U, n, h = hp * UN + u, u // 2, u % 2
                    for half in range(2):
                        if half == 0:
                            pe.wait_ge(s["shift_done"], 2 * U + 2)
                        if not first or u >= 1:
                            pe.wait_ge(s["probs_done"], 2 * U + half - 1)
                        scores(U, u, par, half)
                        if not last and (u, half) in GROUP:
                            project(hp + 1, 1 - par, GROUP[u, half], False)
                        if n >= 1:
                            weigh_values(4 * hp + n - 1, n - 1, par, 2 * h + half, not first or n >= 3)
                        elif not first:
                            weigh_values(4 * hp + n - 1, NB - 1, 1 - par, 2 * h + half, True)
                        if not (last and u >= UN - 2):
                            pe.wait_ge(s["shift_done"], 2 * U + half + 3)
                            if u == UN - 2 and half == 0:
                                if first:
                                    pe.wait_ge(s["consts"], 8)
                                pe.wait_ge(s["q_moved"], 96 * hp + 192)
                                pe.wait_ge(s["k_moved"], 96 * hp + 192)
                            near_scores((u + 2) % UN, par if u < UN - 2 else 1 - par, half)
                        if half == 0:
                            if not (last and u == UN - 1):
                                turn_max(U + 1, (u + 1) % UN, 1)
                        elif not (last and u >= UN - 2):
                            turn_max(U + 2, (u + 2) % UN, 0)

            pe.wait_ge(s["bias_prod"], 2)
            for hp in range(HP):
                pe.matmul(outs[0][:, 0:P], ones[:, :], bvw[:, hp, :], start=(hp == 0), stop=False)
            pe.matmul(outs[0][:, 0:P], ones[0:1, :], bo_row[:, :], start=False, stop=True).then_inc(s["bias_sum"], 1)
            pe.wait_ge(s["bias_out_done"], 1)

            loop_pairs(pe, body)
            for kt in range(KT):
                weigh_values(4 * HP - 1, NB - 1, 1, kt, True)

            for t in range(NT):
                pe.wait_ge(s["oT_done"], 4 * (HP - 1) + t // QT + 1)
                cols = slice(t * P, (t + 1) * P)
                for hp in range(HP):
                    last = three(near[t // 4][:, (t % 4) * P:(t % 4 + 1) * P], oT_hi[:, hp, cols], oT_lo[:, hp, cols],
                                 wo_hi[:, hp, :], wo_lo[:, hp, :], start=(hp == 0), stop=(hp == HP - 1))
                if t % 4 == 3:
                    last.then_inc(s["y_done"], 1)
            for half in range(2):
                turn_x(half, 2 + half)
            pe.wait_ge(s["router_done"], 1)
            pe.wait_ge(s["xT_done"], 4)
            pe.wait_ge(s["attn_done"], 1)
            for t in range(NT):
                cols = slice(t * P, (t + 1) * P)
                last = three(near[0][:, 16 * t:16 * t + NE], xT_hi[:, cols], xT_lo[:, cols], router_hi[:, :], router_lo[:, :])
            last.then_inc(s["logits_done"], 1)

            def gate_up(e, C, c, par, first):
                tc, ft = c // 2, c % 2
                if c == 0:
                    pe.wait_ge(s["wf_done"], 2 * e + 1)
                if not first or c >= 2:
                    pe.wait_ge(s["hid_done"], C - 1)
                cols = slice(tc * 512, (tc + 1) * 512)
                g = slice(ft * P, (ft + 1) * P)
                u = slice((FT + ft) * P, (FT + ft + 1) * P)
                three(score[c % 2][:, :], wf_hi[:, par, g], wf_lo[:, par, g], xT_hi[:, cols], xT_lo[:, cols])
                three(outs[c % 2][:, :], wf_hi[:, par, u], wf_lo[:, par, u], xT_hi[:, cols],
                      xT_lo[:, cols]).then_inc(s["gu_done"], 1)

            def down(e, par, yb, first):
                if yb == 0:
                    pe.wait_ge(s["wf_done"], 2 * e + 2)
                pe.wait_ge(s["hid_lo_done"], 4 * e + 2 * yb + 2)
                if not first:
                    pe.wait_ge(s["summed"], 2 * e - 1 + yb)
                for t in range(4):
                    cols = slice((4 * yb + t) * P, (4 * yb + t + 1) * P)
                    for ft in range(FT):
                        d = slice((2 * FT + ft) * P, (2 * FT + ft + 1) * P)
                        last = three(misc[yb][:, t * P:(t + 1) * P], hid_hi[:, par, ft, cols], hid_lo[:, par, ft, cols],
                                     wf_hi[:, par, d], wf_lo[:, par, d], start=(ft == 0), stop=(ft == FT - 1))
                last.then_inc(s["down_done"], 1)

            def expert(e, par, first, last):
                second = not first and isinstance(e, int) and e == 1
                for c in range(4):
                    gate_up(e, 4 * e + c, c, par, first)
                    if c in (1, 2) and not first:
                        down(e - 1, 1 - par, c - 1, second)

            loop_experts(pe, expert)
            down(NE - 1, 0, 0, False)
            down(NE - 1, 0, 1, False)


def kernel(x, ctx_1024, g_xattn, g_ffn, L0_xattn_Wq, L0_xattn_bq, L0_xattn_Wk, L0_xattn_bk, L0_xattn_Wv,
           L0_xattn_bv, L0_xattn_Wo, L0_xattn_bo, L0_ffn_router_w, L0_ffn_w_gate, L0_ffn_w_up, L0_ffn_w_down,
           L0_ffn_sw_gate, L0_ffn_sw_up, L0_ffn_sw_down, L0_ffn_gate_w):
    import numpy as np
    import concourse.bacc as bacc
    from concourse import mybir as mb
    from concourse.bass_utils import run_bass_kernel_spmd

    a = np.asarray
    x, c = a(x), a(ctx_1024)
    B, Lq, Em = x.shape
    pairs = L0_xattn_Wq.shape[0] // 128
    gate = np.concatenate([a(L0_ffn_w_gate), a(L0_ffn_sw_gate)[None]])
    up = np.concatenate([a(L0_ffn_w_up), a(L0_ffn_sw_up)[None]])
    down = np.concatenate([a(L0_ffn_w_down), a(L0_ffn_sw_down)[None]])
    n_e, F, _ = down.shape
    down = down.reshape(n_e, F // 128, 128, Em).transpose(0, 2, 1, 3).reshape(n_e, 128, -1)
    wqkv = np.stack([a(w).reshape(pairs, 128, Em).transpose(2, 0, 1) for w in (L0_xattn_Wq, L0_xattn_Wk, L0_xattn_Wv)], axis=2)
    data = {
        "xs": x.reshape(B * Lq, Em),
        "ctxT": c.reshape(-1, Em).T,
        "g_xattn": np.broadcast_to(a(g_xattn).reshape(1, 1), (128, 1)),
        "g_ffn": np.broadcast_to(a(g_ffn).reshape(1, 1), (128, 1)),
        "wqkv": wqkv.reshape(Em, pairs, 3 * 128),
        "bqk": np.stack([a(L0_xattn_bq).reshape(pairs, 128).T, a(L0_xattn_bk).reshape(pairs, 128).T], axis=2),
        "bv": a(L0_xattn_bv).reshape(pairs, 128).T,
        "woT": a(L0_xattn_Wo).T,
        "bo": a(L0_xattn_bo).reshape(1, Em),
        "routerT": np.concatenate([a(L0_ffn_router_w), a(L0_ffn_gate_w)]).T,
        "wffn": np.concatenate([gate, up, down], axis=2),
    }
    nc = bacc.Bacc("TRN2", target_bir_lowering=False, num_devices=1)
    arrays, args = {}, {}
    for name, value in data.items():
        value = np.ascontiguousarray(value)
        arrays[name] = value
        args[name] = nc.dram_tensor(name, value.shape, mb.dt.from_np(value.dtype), kind="ExternalInput").ap()
    y = nc.dram_tensor("y", (B * Lq, Em), mb.dt.float32, kind="ExternalOutput").ap()
    flamingo_block(nc, out=y, **args)
    result = run_bass_kernel_spmd(nc, [arrays], core_ids=[0])
    return result.results[0]["y"].reshape(B, Lq, Em)
```

```python
from contextlib import ExitStack

import concourse.bass as bass
from concourse import mybir

P = 128
ALU = mybir.AluOpType
ACT = mybir.ActivationFunctionType
AX = mybir.AxisListType
F32 = mybir.dt.float32
F16 = mybir.dt.float16
BF16 = mybir.dt.bfloat16

ACT_SCALE = 4.0
W_SCALE = 16.0
PROJ_SCALE = ACT_SCALE * W_SCALE
ROW_SCALE = 2048.0
EPS = 1e-5
NEVER = 4.0


def flamingo_block(nc, xs, ctxT, small, wqkv, woT, bo, wffn, out):
    T, E = xs.shape
    HP = wqkv.shape[1]
    NB = 4
    L = T // NB
    S = ctxT.shape[1] // NB
    D = 64
    NT = T // P
    KT = S // P
    QT = L // P
    NE = wffn.shape[0]
    NR = NE - 1
    FT = 2
    UN = 2 * NB
    EXP_SCALE = 1.0 / (8.0 * PROJ_SCALE * PROJ_SCALE)
    HALF = T // 2
    assert E == P and L == 256 and S == 512 and T == 1024 and HP == 8 and NE == 9

    with ExitStack() as ctx:
        def sb(name, shape, dt):
            return ctx.enter_context(nc.sbuf_tensor(name, shape, dt))

        def sem(name):
            return ctx.enter_context(nc.semaphore(name))

        x_in = sb("x_in", [P, NT, P], F32)
        x_norm = sb("x_norm", [P, NT, P], F32)
        x_mid = sb("x_mid", [P, NT, P], F32)
        xT_hi = sb("xT_hi", [P, T], F16)
        xT_lo = sb("xT_lo", [P, T], F16)
        ctx_hi = sb("ctx_hi", [P, NB * S], F16)
        ctx_lo = sb("ctx_lo", [P, NB * S], F16)
        w_qkv = sb("w_qkv", [P, HP, 3 * P], F32)
        w_hi = sb("w_hi", [P, 2, 3 * P], F16)
        w_lo = sb("w_lo", [P, 2, 3 * P], F16)
        wo = sb("wo", [P, HP, P], F32)
        wo_hi = sb("wo_hi", [P, HP, P], F16)
        wo_lo = sb("wo_lo", [P, HP, P], F16)
        cols = sb("cols", [P, 2 + 3 * HP + NE], F32)
        g_col = cols[:, 0:2]
        bias_qk = cols[:, 2:2 + 2 * HP].rearrange("p (h b) -> p h b", b=2)
        bias_v = cols[:, 2 + 2 * HP:2 + 3 * HP]
        router = cols[:, 2 + 3 * HP:2 + 3 * HP + NE]
        bias_pair = sb("bias_pair", [P, 2, 2], F32)
        bo_row = sb("bo_row", [1, P], F32)
        tanh_g = sb("tanh_g", [P, 2], F32)
        attn_gate = sb("attn_gate", [P, 1], F32)
        q_hi = sb("q_hi", [P, T], F16)
        q_lo = sb("q_lo", [P, T], F16)
        k_hi = sb("k_hi", [P, NB * S], F16)
        k_lo = sb("k_lo", [P, NB * S], F16)
        k_both = sb("k_both", [P, 2, 2, NB * S], F16)
        k_row = sb("k_row", [P, 2, 2, NB * S], F16)
        q_twice = sb("q_twice", [P, 2, 2, T], F16)
        q_row = sb("q_row", [P, 2, 2, T], F16)
        v_sb = sb("v_sb", [P, 2, NB * KT, P], F32)
        probs = sb("probs", [P, 4, KT * L], F32)
        part_sum = sb("part_sum", [P, 2 * L], F32)
        prob_sum = sb("prob_sum", [P, 4, L], F32)
        max_cols = sb("max_cols", [P, 2, QT, P], BF16)
        neg_ident = sb("neg_ident", [P, P], BF16)
        ident = sb("ident", [P, P], F32)
        ones = sb("ones", [P, P], F32)
        ln_den = sb("ln_den", [P, L], F32)
        rec_den = sb("rec_den", [P, L], F32)
        den_rec = sb("den_rec", [P, L], F32)
        o_rec = sb("o_rec", [P, L], F32)
        o_norm = sb("o_norm", [P, 2, L], F32)
        oT_hi = sb("oT_hi", [P, HP, T], F16)
        oT_lo = sb("oT_lo", [P, HP, T], F16)
        stats = sb("stats", [P, NT, 6], F32)
        mean_var = sb("mean_var", [P, NT, 2], F32)
        ln_var = sb("ln_var", [P, NT], F32)
        rstd0 = sb("rstd0", [P, NT], F32)
        newton = sb("newton", [P, NT], F32)
        newton2 = sb("newton2", [P, NT], F32)
        ones16 = sb("ones16", [P, D], F16)
        sum_hi = sb("sum_hi", [P, 4, L], F16)
        sum_lo = sb("sum_lo", [P, 4, L], F16)
        rstd = sb("rstd", [P, NT], F32)
        eps_col = sb("eps_col", [P, 1], F32)
        bias_out = sb("bias_out", [P, P], F32)
        router_hi = sb("router_hi", [P, NE], F16)
        router_lo = sb("router_lo", [P, NE], F16)
        logits = sb("logits", [P, NT, NE], F32)
        r_a = sb("r_a", [P, NT, NR], F32)
        r_b = sb("r_b", [P, NT, NR], F32)
        r_c = sb("r_c", [P, NT, NR], F32)
        prob_e = sb("prob_e", [P, NT, NR], F32)
        first_e = sb("first_e", [P, NT, NR], F32)
        order_e = sb("order_e", [P, NR], F32)
        r_m = sb("r_m", [P, NT], F32)
        r_s = sb("r_s", [P, NT], F32)
        gate_e = sb("gate_e", [P, NT], F32)
        mix = sb("mix", [P, NT, NE], F32)
        wf = sb("wf", [P, 2, 768], F32)

        ctx32 = probs[:, 0:2, :].rearrange("p a b -> p (a b)")
        bvw = v_sb[:, 1, 0:HP, :]
        silu = probs[:, 0, :].rearrange("p (a b) -> p a b", a=2)
        hid = probs[:, 1:3, :].rearrange("p s (a b) -> p (s a) b", a=2)
        hid_hi = k_both[:, 0, :, :].rearrange("p a (f t) -> p a f t", f=FT)
        hid_lo = k_both[:, 1, :, :].rearrange("p a (f t) -> p a f t", f=FT)
        wf_hi = k_hi[:, 0:1536].rearrange("p (a b) -> p a b", a=2)
        wf_lo = k_lo[:, 0:1536].rearrange("p (a b) -> p a b", a=2)

        banks = [ctx.enter_context(nc.psum_tensor(f"bank{i}", [P, 512], F32)) for i in range(8)]
        near = [banks[0], banks[1]]
        score = [banks[2], banks[3]]
        outs = [banks[4], banks[5]]
        misc = [banks[6], banks[7]]

        names = """x0_loaded x1_loaded ctx0_loaded ctx1_loaded ctx2_loaded ctx3_loaded w_first_loaded
        w_rest_loaded cols_loaded bo_loaded wo_loaded wf0_loaded wf1_loaded consts
        pool_step stats_done var_ready ln_half rstd_done normed transposed xT_hi_done xT_done
        ctx_hi_done ctx_done w_hi_done w_done bias_done wo_hi_done wo_done bias_prod bias_sum bias_out_done
        projected hi_done lo_done v_done start_near0 start_near1 start_row0 start_row1 rest_q0 rest_q1
        rest_q_row q_moved k0_moved k1_moved row_moved near_done max_done shift_made shift_done
        scores_done probs_done sums_half sums_done sum_hi_done sum_lo_done values_done pv_done ln_done
        rec_done div_half psum_read div_done
        oT_hi_done oT_done y_done stats_half attn_done router_done logits_done route route_exp route_act
        mix_done wf_hi_done wf_done gu_done silu_done hid_done hid_hi_done hid_lo_done down_done
        summed stored tanh_done gate_ready mid_start router_hi_done""".split()
        s = {n: sem(n) for n in names}
        block = ctx.enter_context(nc.Block())

        GROUP = {(1, 0): 0, (1, 1): 1, (2, 0): 2, (2, 1): 3, (3, 0): 4, (3, 1): 5, (4, 0): 6, (5, 0): 7,
                 (5, 1): 8, (7, 0): 9}

        FIRST_ORDER = (2, 0, 3, 4, 5, 1, 6, 7, 8, 9)

        OUT_BANKS = (misc[0], misc[1], score[0], score[1])

        def group_bank(j, first):
            return (misc + score)[j % 4] if first else misc[j % 2]

        def loop_pairs(eng, body):
            body(0, 0, True, False)
            with eng.Fori(0, (HP - 2) // 2) as i:
                body(2 * i + 1, 1, False, False)
                body(2 * i + 2, 0, False, False)
            body(HP - 1, 1, False, True)

        GU_BANKS = ((banks[2], banks[4]), (banks[3], banks[5]), (banks[0], banks[1]))
        GU_SLOT = ((0, 1, 2, 1), (0, 2, 1, 2))
        GU_BACK = (4, 3, 3, 2)

        LAST_DOWN = ((range(0, 4), misc[0]), (range(4, 6), misc[1]), (range(6, 8), banks[0]))

        def loop_experts(eng, body):
            body(0, 0, True, False)
            body(1, 1, False, False)
            with eng.Fori(0, (NE - 3) // 2) as i:
                body(2 * i + 2, 0, False, False)
                body(2 * i + 3, 1, False, False)
            body(NE - 1, 0, False, True)

        @block.sync
        def _(sp):
            xv = xs.rearrange("(t p) e -> p t e", p=P)
            def load_x(h):
                sp.dma_start(x_in[:, 4 * h:4 * h + 4, :], xv[:, 4 * h:4 * h + 4, :]).then_inc(s[f"x{h}_loaded"], 16)

            def load_ctx(n):
                sp.dma_start(ctx32[:, n * S:(n + 1) * S], ctxT[:, n * S:(n + 1) * S]).then_inc(s[f"ctx{n}_loaded"], 16)

            load_x(0)
            sp.dma_start(w_qkv[:, 0:1, :], wqkv[:, 0:1, :]).then_inc(s["w_first_loaded"], 16)
            load_ctx(0)
            load_x(1)
            for n in range(1, NB):
                load_ctx(n)
            sp.dma_start(wo[:, :, :], woT.rearrange("(h p) e -> p h e", p=P)).then_inc(s["wo_loaded"], 16)
            sp.dma_start(bo_row[:, :], bo).then_inc(s["bo_loaded"], 16)
            sp.dma_start(w_qkv[:, 1:HP, :], wqkv[:, 1:HP, :]).then_inc(s["w_rest_loaded"], 16)
            for e in range(2):
                sp.dma_start(wf[:, e, :], wffn[e]).then_inc(s[f"wf{e}_loaded"], 16)

            sp.wait_ge(s["lo_done"], 1)
            for h in range(2):
                rows = slice(D * h, D * h + D)
                sp.dma_start(k_both[0:D, 0, h, 0:S], k_hi[rows, 0:S]).then_inc(s[f"start_near{h}"], 16)
                sp.dma_start(k_both[D:P, 0, h, 0:S], k_lo[rows, 0:S]).then_inc(s[f"start_near{h}"], 16)
                if h == 0:
                    sp.wait_ge(s["lo_done"], 2)
                for half in (slice(0, D), slice(D, P)):
                    sp.dma_start(q_twice[half, 0, h, 0:HALF], q_hi[rows, 0:HALF]).then_inc(s[f"start_near{h}"], 16)
            sp.wait_ge(s["lo_done"], 5)
            for h in range(2):
                rows = slice(D * h, D * h + D)
                sp.dma_start(k_both[0:D, 0, h, S:], k_hi[rows, S:]).then_inc(s[f"k{h}_moved"], 16)
                sp.dma_start(k_both[D:P, 0, h, S:], k_lo[rows, S:]).then_inc(s[f"k{h}_moved"], 16)
            for h in range(2):
                rows = slice(D * h, D * h + D)
                sp.dma_start(k_row[0:D, 0, h, S:], k_hi[rows, S:]).then_inc(s["row_moved"], 16)
            sp.wait_ge(s["lo_done"], 6)
            for h in range(2):
                rows = slice(D * h, D * h + D)
                sp.dma_start(q_twice[0:D, 0, h, HALF:], q_hi[rows, HALF:]).then_inc(s[f"rest_q{h}"], 16)
                sp.dma_start(q_twice[D:P, 0, h, HALF:], q_hi[rows, HALF:]).then_inc(s[f"rest_q{h}"], 16)

            def move(hp1, par1, first):
                sp.wait_ge(s["lo_done"], 6 * hp1 + 2)
                if not first:
                    sp.wait_ge(s["scores_done"], 16 * hp1 - 16)
                for h in range(2):
                    rows = slice(D * h, D * h + D)
                    sp.dma_start(q_twice[0:D, par1, h, :], q_hi[rows, :]).then_inc(s["q_moved"], 16)
                    sp.dma_start(q_twice[D:P, par1, h, :], q_hi[rows, :]).then_inc(s["q_moved"], 16)
                    sp.dma_start(q_row[0:D, par1, h, :], q_lo[rows, :]).then_inc(s["q_moved"], 16)
                sp.wait_ge(s["lo_done"], 6 * hp1 + 6)
                for h in range(2):
                    rows = slice(D * h, D * h + D)
                    sp.dma_start(k_both[0:D, par1, h, :], k_hi[rows, :]).then_inc(s[f"k{h}_moved"], 16)
                    sp.dma_start(k_both[D:P, par1, h, :], k_lo[rows, :]).then_inc(s[f"k{h}_moved"], 16)
                for h in range(2):
                    rows = slice(D * h, D * h + D)
                    sp.dma_start(k_row[0:D, par1, h, :], k_hi[rows, :]).then_inc(s["row_moved"], 16)

            move(1, 1, True)
            with sp.Fori(0, (HP - 2) // 2) as i:
                move(2 * i + 2, 0, False)
                move(2 * i + 3, 1, False)

            def load_expert(e, par):
                sp.wait_ge(s["wf_done"], 2 * e - 2)
                sp.dma_start(wf[:, par:par + 1, :], wffn[bass.ds(e, 1)].rearrange("e p f -> p e f")).then_inc(s[f"wf{par}_loaded"], 16)

            with sp.Fori(0, 3) as i:
                load_expert(2 * i + 2, 0)
                load_expert(2 * i + 3, 1)
            load_expert(NE - 1, 0)

            ov = out.rearrange("(t p) e -> p t e", p=P)
            for part, tiles in enumerate((slice(0, 4), slice(4, 6), slice(6, 8))):
                sp.wait_ge(s["summed"], 2 * NE - 1 + part)
                sp.dma_start(ov[:, tiles, :], x_mid[:, tiles, :]).then_inc(s["stored"], 16)
            sp.wait_ge(s["stored"], 48)

        @block.gpsimd
        def _(pool):
            pool.memset(ident[:, :], 0.0).then_inc(s["pool_step"], 1)
            pool.memset(neg_ident[:, :], 0.0).then_inc(s["pool_step"], 1)
            pool.wait_ge(s["pool_step"], 2)
            pool.affine_select(out=ident[:, :], in_=ident[:, :], compare_op=ALU.not_equal, fill=1.0, base=0,
                               pattern=[[-1, P]], channel_multiplier=1).then_inc(s["consts"], 1)
            pool.affine_select(out=neg_ident[:, :], in_=neg_ident[:, :], compare_op=ALU.not_equal,
                               fill=-1.0 / ROW_SCALE, base=0, pattern=[[-1, P]], channel_multiplier=1).then_inc(s["consts"], 1)
            pool.memset(max_cols[:, :, :, :], 0.0).then_inc(s["consts"], 1)
            pool.memset(ones16[:, :], 1.0)
            pool.memset(ones[:, :], 1.0).then_inc(s["consts"], 1)
            pool.wait_ge(s["consts"], 4)
            for par in range(2):
                pool.memset(k_row[D:D + 1, par, :, :], ROW_SCALE).then_inc(s["consts"], 1)
            pool.wait_ge(s["consts"], 6)
            for e in range(NR):
                last = pool.memset(order_e[:, e:e + 1], float(NR - e))
            last.then_inc(s["consts"], 1)
            pool.wait_ge(s["wo_loaded"], 16)
            pool.wait_ge(s["cols_loaded"], 16)
            pool.tensor_tensor(bvw, wo[:, :, :], bias_v.unsqueeze(2).broadcast_to([P, HP, P]), ALU.mult).then_inc(s["bias_prod"], 1)
            for step, m in enumerate((HP // 2, HP // 4, HP // 8)):
                pool.wait_ge(s["bias_prod"], step + 1)
                pool.tensor_tensor(bvw[:, 0:m, :], bvw[:, 0:m, :], bvw[:, m:2 * m, :], ALU.add).then_inc(s["bias_prod"], 1)

            def low_sums(m, n):
                pool.wait_ge(s["sum_hi_done"], m + 1)
                slots = slice(n % 2 * 2, n % 2 * 2 + 2)
                pool.tensor_tensor(sum_lo[:, slots, :], prob_sum[:, slots, :], sum_hi[:, slots, :],
                                   ALU.subtract).then_inc(s["sum_lo_done"], 1)

            pool.wait_ge(s["lo_done"], 2)
            for h in range(2):
                rows = slice(D * h, D * h + D)
                pool.dma_start(k_row[0:D, 0, h, 0:S], k_hi[rows, 0:S]).then_inc(s[f"start_row{h}"], 16)
                pool.dma_start(q_row[0:D, 0, h, 0:HALF], q_lo[rows, 0:HALF]).then_inc(s[f"start_row{h}"], 16)
            pool.wait_ge(s["lo_done"], 6)
            for h in range(2):
                pool.dma_start(q_row[0:D, 0, h, HALF:], q_lo[D * h:D * h + D, HALF:]).then_inc(s["rest_q_row"], 16)

            def low_o(m, hp, n):
                pool.wait_ge(s["oT_hi_done"], m + 1)
                pool.tensor_tensor(oT_lo[:, bass.ds(hp, 1), n * L:(n + 1) * L], o_norm[:, n % 2:n % 2 + 1, :],
                                   oT_hi[:, bass.ds(hp, 1), n * L:(n + 1) * L], ALU.subtract).then_inc(s["oT_done"], 1)

            def body(hp, par, first, last):
                for u in range(UN):
                    U, n, slot = hp * UN + u, u // 2, (u // 2) % 2 * 2 + u % 2
                    if u % 2 == 1 and (not first or n >= 1):
                        low_sums(4 * hp + n - 1, (n - 1) % 2)
                    if not first or u >= 1:
                        pool.wait_ge(s["sums_done"], U)
                    pool.wait_ge(s["probs_done"], 2 * U + 2)
                    pool.tensor_tensor(part_sum[:, :], probs[:, slot, 0:2 * L], probs[:, slot, 2 * L:4 * L],
                                       ALU.add).then_inc(s["sums_half"], 1)
                    pool.wait_ge(s["sums_half"], U + 1)
                    if u % 2 == 0 and (not first or n >= 2):
                        pool.wait_ge(s["sum_lo_done"], 4 * hp + n - 1)
                    pool.tensor_tensor(prob_sum[:, slot, :], part_sum[:, 0:L], part_sum[:, L:2 * L],
                                       ALU.add).then_inc(s["sums_done"], 1)
                    if u % 2 == 1:
                        if n >= 2:
                            low_o(4 * hp + n - 2, hp, n - 2)
                        elif not first:
                            low_o(4 * hp + n - 2, hp - 1, n + 2)

            loop_pairs(pool, body)
            low_o(4 * HP - 2, HP - 1, 2)
            low_o(4 * HP - 1, HP - 1, 3)

            def expert(e, par, first, last):
                for c in range(4):
                    C, tc, ft = 4 * e + c, c // 2, c % 2
                    pool.wait_ge(s["hid_hi_done"], C + 1)
                    pool.tensor_tensor(hid_lo[:, par, ft, tc * 512:(tc + 1) * 512], hid[:, c, :],
                                       hid_hi[:, par, ft, tc * 512:(tc + 1) * 512], ALU.subtract).then_inc(s["hid_lo_done"], 1)

            loop_experts(pool, expert)

        @block.scalar
        def _(act):
            act.dma_start(cols[:, :], small).then_inc(s["cols_loaded"], 16)
            act.wait_ge(s["cols_loaded"], 16)
            act.activation(tanh_g[:, :], g_col, ACT.Tanh).then_inc(s["tanh_done"], 1)
            act.preload_act_table_set("natural_log_exp_and_others")

            def split_w(hp, par):
                act.activation(w_hi[:, par:par + 1, :], w_qkv[:, bass.ds(hp, 1), :], ACT.Copy,
                               scale=W_SCALE).then_inc(s["w_hi_done"], 1)

            def rstd_guess(half, at):
                act.wait_ge(s["stats_done"], at + 1)
                act.activation(ln_var[:, 4 * half:4 * half + 4], mean_var[:, 4 * half:4 * half + 4, 1], ACT.Ln,
                               bias=eps_col[:, 0:1]).then_inc(s["ln_half"], 1)
                act.wait_ge(s["ln_half"], at + 1)
                act.activation(rstd0[:, 4 * half:4 * half + 4], ln_var[:, 4 * half:4 * half + 4], ACT.Exp,
                               scale=-0.5).then_inc(s["var_ready"], 1)

            def high_x(half, at):
                act.wait_ge(s["transposed"], at + 1)
                act.activation(xT_hi[:, half * HALF:(half + 1) * HALF], (outs if at < 2 else misc)[half][:, :],
                               ACT.Copy).then_inc(s["xT_hi_done"], 1)

            def high_ctx(n):
                act.wait_ge(s[f"ctx{n}_loaded"], 16)
                act.activation(ctx_hi[:, n * S:(n + 1) * S], ctx32[:, n * S:(n + 1) * S], ACT.Copy,
                               scale=ACT_SCALE).then_inc(s["ctx_hi_done"], 1)

            def evacuate(hp1, par1, j, g, first, after_first=False):
                act.wait_ge(s["projected"], 10 * hp1 + j + 1)
                if j == 0:
                    act.wait_ge(s["bias_done"], hp1 + 1)
                if g < 2:
                    if g == 0 and not first:
                        if after_first:
                            for name in ("rest_q0", "rest_q1", "rest_q_row"):
                                act.wait_ge(s[name], 32)
                        else:
                            act.wait_ge(s["q_moved"], 96 * hp1 - 96)
                    act.activation(q_hi[:, g * 512:(g + 1) * 512], group_bank(j, first)[:, :], ACT.Identity,
                                   bias=bias_pair[:, par1, 0:1]).then_inc(s["hi_done"], 1)
                elif g < 6:
                    if g == 2 and not first:
                        act.wait_ge(s["k0_moved"], 32 * hp1)
                        act.wait_ge(s["k1_moved"], 32 * hp1)
                        act.wait_ge(s["row_moved"], 32 * hp1)
                    act.activation(k_hi[:, (g - 2) * 512:(g - 1) * 512], group_bank(j, first)[:, :], ACT.Identity,
                                   bias=bias_pair[:, par1, 1:2]).then_inc(s["hi_done"], 1)
                else:
                    act.activation(v_sb[:, par1, (g - 6) * KT:(g - 5) * KT, :], group_bank(j, first)[:, :].rearrange("p (a b) -> p a b", a=KT),
                                   ACT.Copy).then_inc(s["v_done"], 1)

            def place_shift(U, u, par, qt):
                act.wait_ge(s["shift_made"], 2 * U + qt + 1)
                at = u // 2 * L + qt * P
                act.activation(q_row[D:D + 1, par, u % 2, at:at + P], near[qt][D:D + 1, 0:P],
                               ACT.Copy).then_inc(s["shift_done"], 1)

            def reciprocal_guess(m, n, first=False):
                if not first:
                    act.wait_ge(s["psum_read"], m)
                act.wait_ge(s["pv_done"], m + 1)
                act.activation(ln_den[:, :], outs[n % 2][:, L:2 * L], ACT.Ln).then_inc(s["ln_done"], 1)
                act.wait_ge(s["ln_done"], m + 1)
                act.activation(rec_den[:, :], ln_den[:, :], ACT.Exp, scale=-1.0).then_inc(s["rec_done"], 1)

            def high_o(m, hp, n):
                act.wait_ge(s["div_done"], m + 1)
                act.activation(oT_hi[:, bass.ds(hp, 1), n * L:(n + 1) * L], o_norm[:, n % 2:n % 2 + 1, :],
                               ACT.Copy).then_inc(s["oT_hi_done"], 1)

            rstd_guess(0, 0)
            act.wait_ge(s["w_first_loaded"], 16)
            split_w(0, 0)
            high_ctx(0)
            high_x(0, 0)
            high_ctx(1)
            evacuate(0, 0, 0, FIRST_ORDER[0], True)
            high_ctx(2)
            evacuate(0, 0, 1, FIRST_ORDER[1], True)
            rstd_guess(1, 1)
            evacuate(0, 0, 2, FIRST_ORDER[2], True)
            high_ctx(3)
            evacuate(0, 0, 3, FIRST_ORDER[3], True)
            high_x(1, 1)
            for j in range(4, 8):
                evacuate(0, 0, j, FIRST_ORDER[j], True)
            for qt in range(QT):
                place_shift(0, 0, 0, qt)
                evacuate(0, 0, 8 + qt, FIRST_ORDER[8 + qt], True)

            def split_gate_up(e, par):
                act.wait_ge(s[f"wf{par}_loaded"], 8 * (e - par) + 16)
                act.activation(wf_hi[:, par, 0:512], wf[:, par, 0:512], ACT.Copy, scale=W_SCALE).then_inc(s["wf_hi_done"], 1)

            def split_down(par):
                act.activation(wf_hi[:, par, 512:768], wf[:, par, 512:768], ACT.Copy, scale=W_SCALE).then_inc(s["wf_hi_done"], 1)

            def high_sums(m, n):
                act.wait_ge(s["sums_done"], 2 * m + 2)
                slots = slice(n % 2 * 2, n % 2 * 2 + 2)
                act.activation(sum_hi[:, slots, :], prob_sum[:, slots, :], ACT.Copy).then_inc(s["sum_hi_done"], 1)

            def body(hp, par, first, last):
                for u in range(UN):
                    U, n, h = hp * UN + u, u // 2, u % 2
                    slot = n % 2 * 2 + h
                    if u == 0 and not last:
                        if first:
                            act.wait_ge(s["w_rest_loaded"], 16)
                        split_w(hp + 1, 1 - par)
                    if first and u == 5:
                        act.wait_ge(s["wo_loaded"], 16)
                        act.activation(wo_hi[:, :, :], wo[:, :, :], ACT.Copy, scale=W_SCALE).then_inc(s["wo_hi_done"], 1)
                        act.activation(router_hi[:, :], router, ACT.Copy, scale=W_SCALE).then_inc(s["router_hi_done"], 1)
                    if last and u == 2:
                        act.wait_ge(s["k0_moved"], 32 * HP)
                        act.wait_ge(s["k1_moved"], 32 * HP)
                        act.wait_ge(s["row_moved"], 32 * HP)
                        for e in range(2):
                            split_gate_up(e, e)
                            split_down(e)
                    for half in range(2):
                        if u < UN - 1:
                            place_shift(U + 1, u + 1, par, half)
                        elif not last:
                            place_shift(U + 1, 0, 1 - par, half)
                        act.wait_ge(s["scores_done"], 2 * U + half + 1)
                        if half == 0 and (not first or n >= 2):
                            act.wait_ge(s["values_done"], 4 * hp + n - 1)
                        act.activation(probs[:, slot, half * 512:(half + 1) * 512], score[half][:, :], ACT.Exp,
                                       scale=EXP_SCALE).then_inc(s["probs_done"], 1)
                        if not last and (u, half) in GROUP:
                            evacuate(hp + 1, 1 - par, GROUP[u, half], GROUP[u, half], False, first)
                        if (h, half) == (1, 0) and (not first or n >= 1):
                            high_sums(4 * hp + n - 1, (n - 1) % 2)
                        if not first or n >= 2:
                            if (h, half) == (0, 1):
                                reciprocal_guess(4 * hp + n - 2, n % 2, first and n == 2)
                        if (h, half) == (0, 0):
                            if n >= 3:
                                high_o(4 * hp + n - 3, hp, n - 3)
                            elif not first:
                                high_o(4 * hp + n - 3, hp - 1, n + 1)

            loop_pairs(act, body)
            high_o(4 * HP - 3, HP - 1, 1)
            reciprocal_guess(4 * HP - 2, 0)
            high_sums(4 * HP - 1, 1)
            high_o(4 * HP - 2, HP - 1, 2)
            reciprocal_guess(4 * HP - 1, 1)
            rstd_guess(0, 2)
            high_o(4 * HP - 1, HP - 1, 3)
            high_x(0, 2)
            rstd_guess(1, 3)
            act.preload_act_table_set("silu_and_others")

            def high_hidden(C, par, c):
                act.wait_ge(s["hid_done"], C + 1)
                act.activation(hid_hi[:, par, c % 2, (c // 2) * 512:(c // 2 + 1) * 512], hid[:, c, :],
                               ACT.Copy).then_inc(s["hid_hi_done"], 1)

            def expert(e, par, first, last):
                for c in range(4):
                    C = 4 * e + c
                    act.wait_ge(s["gu_done"], C + 1)
                    if not first or c >= 2:
                        act.wait_ge(s["hid_done"], C - 1)
                    act.activation(silu[:, c % 2, :], GU_BANKS[GU_SLOT[par][c]][0][:, :], ACT.Silu, scale=1.0 / PROJ_SCALE).then_inc(s["silu_done"], 1)
                    if c == 0:
                        if not first:
                            high_hidden(C - 1, 1 - par, 3)
                        else:
                            high_x(1, 3)
                    else:
                        if c == 1 and not first:
                            act.wait_ge(s["down_done"], 2 * e - 2)
                        high_hidden(C - 1, par, c - 1)
                    if c == 1 and first:
                        act.wait_ge(s["route_exp"], 1)
                        act.activation(r_b[:, :, :], r_a[:, :, :], ACT.Exp).then_inc(s["route_act"], 1)
                        act.activation(gate_e[:, :], logits[:, :, NR], ACT.Exp, scale=-1.0).then_inc(s["route_act"], 1)
                        act.preload_act_table_set("silu_and_others")
                    if c == 1 and not first and not last:
                        split_gate_up(e + 1, 1 - par)
                    if c == 3 and not first and not last:
                        act.wait_ge(s["down_done"], 2 * e)
                        split_down(1 - par)

            loop_experts(act, expert)
            high_hidden(4 * NE - 1, 0, 3)

        @block.vector
        def _(dve):
            dve.memset(eps_col[:, :], EPS)

            def layer_stats(src, tiles, at):
                for t in tiles:
                    dve.bn_stats(stats[:, t, :], src[:, t, :]).then_inc(s["stats_half"], 1)
                for j, t in enumerate(tiles):
                    dve.wait_ge(s["stats_half"], at + j + 1)
                    last = dve.bn_aggr(mean_var[:, t, :], stats[:, t, :])
                return last

            def layer_norm(src, half, at):
                hs = slice(4 * half, 4 * half + 4)
                step = 3 * at
                dve.wait_ge(s["var_ready"], at + 1)
                dve.wait_ge(s["stats_done"], at + 1)
                dve.scalar_tensor_tensor(newton[:, hs], mean_var[:, hs, 1], EPS, rstd0[:, hs], ALU.add,
                                         ALU.mult).then_inc(s["rstd_done"], 1)
                dve.wait_ge(s["rstd_done"], step + 1)
                dve.scalar_tensor_tensor(newton2[:, hs], newton[:, hs], -0.5 * ACT_SCALE, rstd0[:, hs], ALU.mult,
                                         ALU.mult).then_inc(s["rstd_done"], 1)
                dve.wait_ge(s["rstd_done"], step + 2)
                dve.scalar_tensor_tensor(rstd[:, hs], newton2[:, hs], 1.5 * ACT_SCALE, rstd0[:, hs], ALU.add,
                                         ALU.mult).then_inc(s["rstd_done"], 1)
                dve.wait_ge(s["rstd_done"], step + 3)
                for t in range(4 * half, 4 * half + 4):
                    dve.tensor_scalar(x_norm[:, t, :], src[:, t, :], mean_var[:, t, 0:1], rstd[:, t:t + 1],
                                      ALU.subtract, ALU.mult).then_inc(s["normed"], 1)

            def low_x(half, at):
                dve.wait_ge(s["xT_hi_done"], at + 1)
                dve.tensor_tensor(xT_lo[:, half * HALF:(half + 1) * HALF], (outs if at < 2 else misc)[half][:, :],
                                  xT_hi[:, half * HALF:(half + 1) * HALF], ALU.subtract).then_inc(s["xT_done"], 1)

            def low_w(hp, par):
                dve.tensor_scalar(bias_pair[:, par:par + 1, :], bias_qk[:, bass.ds(hp, 1), :], PROJ_SCALE, None,
                                  ALU.mult).then_inc(s["bias_done"], 1)
                dve.wait_ge(s["w_hi_done"], hp + 1)
                dve.scalar_tensor_tensor(w_lo[:, par:par + 1, :], w_qkv[:, bass.ds(hp, 1), :], W_SCALE,
                                         w_hi[:, par:par + 1, :], ALU.mult, ALU.subtract).then_inc(s["w_done"], 1)

            def low_ctx(n):
                dve.wait_ge(s["ctx_hi_done"], n + 1)
                dve.scalar_tensor_tensor(ctx_lo[:, n * S:(n + 1) * S], ctx32[:, n * S:(n + 1) * S], ACT_SCALE,
                                         ctx_hi[:, n * S:(n + 1) * S], ALU.mult, ALU.subtract).then_inc(s["ctx_done"], 1)

            def low_part(hp1, par1, j, g, first=False):
                dve.wait_ge(s["hi_done"], 6 * hp1 + j + 1)
                if j == 0:
                    dve.wait_ge(s["bias_done"], hp1 + 1)
                if g < 2:
                    lo, hi, b, at = q_lo, q_hi, bias_pair[:, par1, 0:1], g * 512
                else:
                    lo, hi, b, at = k_lo, k_hi, bias_pair[:, par1, 1:2], (g - 2) * 512
                dve.scalar_tensor_tensor(lo[:, at:at + 512], group_bank(j, first)[:, :], b, hi[:, at:at + 512],
                                         ALU.add, ALU.subtract).then_inc(s["lo_done"], 1)

            def take_max(U, u, qt, first):
                dve.wait_ge(s["near_done"], 2 * U + qt + 1)
                if not first:
                    dve.wait_ge(s["shift_made"], 2 * U + qt - 3)
                dve.tensor_reduce(max_cols[:, u % 2, qt, D:D + 1], near[qt][:, :], AX.X, ALU.max).then_inc(s["max_done"], 1)

            def divide(m, n, first=False):
                if not first:
                    dve.wait_ge(s["div_done"], m)
                dve.wait_ge(s["rec_done"], m + 1)
                dve.tensor_tensor(den_rec[:, :], outs[n % 2][:, L:2 * L], rec_den[:, :], ALU.mult).then_inc(s["div_half"], 1)
                dve.tensor_tensor(o_rec[:, :], outs[n % 2][:, 0:L], rec_den[:, :], ALU.mult).then_inc(s["psum_read"], 1)
                dve.wait_ge(s["div_half"], m + 1)
                dve.wait_ge(s["psum_read"], m + 1)
                dve.scalar_tensor_tensor(o_norm[:, n % 2, :], den_rec[:, :], -2.0, o_rec[:, :], ALU.add,
                                         ALU.mult).then_inc(s["div_done"], 1)

            def low_gate_up(e, par):
                dve.wait_ge(s["wf_hi_done"], 2 * e + 1)
                dve.scalar_tensor_tensor(wf_lo[:, par, 0:512], wf[:, par, 0:512], W_SCALE, wf_hi[:, par, 0:512],
                                         ALU.mult, ALU.subtract).then_inc(s["wf_done"], 1)

            def low_down(e, par):
                dve.wait_ge(s["wf_hi_done"], 2 * e + 2)
                dve.scalar_tensor_tensor(wf_lo[:, par, 512:768], wf[:, par, 512:768], W_SCALE, wf_hi[:, par, 512:768],
                                         ALU.mult, ALU.subtract).then_inc(s["wf_done"], 1)

            dve.wait_ge(s["x0_loaded"], 16)
            layer_stats(x_in, range(0, 4), 0).then_inc(s["stats_done"], 1)
            layer_norm(x_in, 0, 0)
            dve.wait_ge(s["cols_loaded"], 16)
            low_w(0, 0)
            low_ctx(0)
            low_x(0, 0)
            low_ctx(1)
            dve.wait_ge(s["x1_loaded"], 16)
            layer_stats(x_in, range(4, 8), 4).then_inc(s["stats_done"], 1)
            low_part(0, 0, 0, FIRST_ORDER[0], True)
            low_part(0, 0, 1, FIRST_ORDER[1], True)
            low_ctx(2)
            low_part(0, 0, 2, FIRST_ORDER[2], True)
            layer_norm(x_in, 1, 1)
            low_ctx(3)
            low_part(0, 0, 3, FIRST_ORDER[3], True)
            low_x(1, 1)
            for j in range(4, 6):
                low_part(0, 0, j, FIRST_ORDER[j], True)
            dve.wait_ge(s["consts"], 4)
            for i in range(4):
                take_max(i // 2, i // 2, i % 2, True)
            dve.wait_ge(s["bias_sum"], 1)
            dve.tensor_copy(bias_out[:, :], outs[0][:, 0:P]).then_inc(s["bias_out_done"], 1)

            def body(hp, par, first, last):
                for u in range(UN):
                    U, n, h = hp * UN + u, u // 2, u % 2
                    if u == 0 and not last:
                        low_w(hp + 1, 1 - par)
                    if last and u == 1:
                        dve.wait_ge(s["tanh_done"], 1)
                        dve.wait_ge(s["bias_out_done"], 1)
                        dve.tensor_scalar(attn_gate[:, :], tanh_g[:, 0:1], -1.0 / (PROJ_SCALE * W_SCALE), None,
                                          ALU.mult).then_inc(s["gate_ready"], 1)
                        dve.scalar_tensor_tensor(x_mid[:, :, :], bias_out[:, :].unsqueeze(1).broadcast_to([P, NT, P]),
                                                 tanh_g[:, 0:1], x_in[:, :, :], ALU.mult, ALU.add).then_inc(s["mid_start"], 1)
                    if first and u == 6:
                        dve.wait_ge(s["wo_hi_done"], 1)
                        dve.scalar_tensor_tensor(wo_lo[:, :, :], wo[:, :, :], W_SCALE, wo_hi[:, :, :], ALU.mult,
                                                 ALU.subtract).then_inc(s["wo_done"], 1)
                        dve.wait_ge(s["router_hi_done"], 1)
                        dve.scalar_tensor_tensor(router_lo[:, :], router, W_SCALE, router_hi[:, :], ALU.mult,
                                                 ALU.subtract).then_inc(s["router_done"], 1)
                    if last and u == 4:
                        for e in range(2):
                            low_gate_up(e, e)
                            low_down(e, e)
                    for half in range(2):
                        if not (last and u >= UN - 2):
                            take_max(U + 2, u, half, False)
                        if not last and GROUP.get((u, half), 9) < 6:
                            low_part(hp + 1, 1 - par, GROUP[u, half], GROUP[u, half])
                        if (h, half) == (0, 1) and (not first or n >= 2):
                            if not first:
                                dve.wait_ge(s["oT_done"], 4 * hp + n - 3)
                            divide(4 * hp + n - 2, n % 2, first and n == 2)

            loop_pairs(dve, body)
            dve.wait_ge(s["gate_ready"], 1)
            dve.wait_ge(s["mid_start"], 1)

            def add_attention(quarter):
                qs = slice(2 * quarter, 2 * quarter + 2)
                dve.wait_ge(s["y_done"], quarter + 1)
                y = OUT_BANKS[quarter][:, 0:2 * P].rearrange("p (a b) -> p a b", a=2)
                dve.scalar_tensor_tensor(x_mid[:, qs, :], y, attn_gate[:, 0:1], x_mid[:, qs, :], ALU.mult,
                                         ALU.add).then_inc(s["attn_done"], 1)
                dve.wait_ge(s["attn_done"], quarter + 1)
                return layer_stats(x_mid, range(2 * quarter, 2 * quarter + 2), 8 + 2 * quarter)

            add_attention(0)
            dve.wait_ge(s["oT_done"], 4 * HP - 3)
            divide(4 * HP - 2, 0)
            dve.wait_ge(s["sum_hi_done"], 4 * HP)
            dve.tensor_tensor(sum_lo[:, 2:4, :], prob_sum[:, 2:4, :], sum_hi[:, 2:4, :],
                              ALU.subtract).then_inc(s["sum_lo_done"], 1)
            add_attention(1).then_inc(s["stats_done"], 1)
            dve.wait_ge(s["oT_done"], 4 * HP - 2)
            divide(4 * HP - 1, 1)
            layer_norm(x_mid, 0, 2)
            add_attention(2)
            low_x(0, 2)
            add_attention(3).then_inc(s["stats_done"], 1)
            layer_norm(x_mid, 1, 3)

            count = [0]

            def link(ins):
                count[0] += 1
                ins.then_inc(s["route"], 1)
                dve.wait_ge(s["route"], count[0])

            def over_experts(col):
                return col[:, :].unsqueeze(2).broadcast_to([P, NT, NR])

            order = order_e[:, :].unsqueeze(1).broadcast_to([P, NT, NR])

            def route_logits():
                dve.wait_ge(s["logits_done"], 2)
                link(dve.tensor_scalar(logits[:, :, :], misc[0][:, 0:16 * NT].rearrange("p (t e) -> p t e", e=16)[:, :, 0:NE],
                                       1.0 / PROJ_SCALE, None, ALU.mult))
                link(dve.tensor_reduce(r_m[:, :], logits[:, :, 0:NR], AX.X, ALU.max))
                dve.tensor_tensor(r_a[:, :, :], logits[:, :, 0:NR], over_experts(r_m), ALU.subtract).then_inc(s["route_exp"], 1)

            def route_softmax():
                dve.wait_ge(s["route_act"], 2)
                link(dve.tensor_reduce(r_s[:, :], r_b[:, :, :], AX.X, ALU.add))
                link(dve.reciprocal(r_m[:, :], r_s[:, :]))
                link(dve.tensor_tensor(prob_e[:, :, :], r_b[:, :, :], over_experts(r_m), ALU.mult))

            def pick(dst, src):
                link(dve.tensor_reduce(r_m[:, :], src[:, :, :], AX.X, ALU.max))
                link(dve.tensor_tensor(r_a[:, :, :], src[:, :, :], over_experts(r_m), ALU.is_ge))
                link(dve.tensor_tensor(r_b[:, :, :], r_a[:, :, :], order, ALU.mult))
                link(dve.tensor_reduce(r_s[:, :], r_b[:, :, :], AX.X, ALU.max))
                link(dve.tensor_tensor(dst[:, :, :], r_b[:, :, :], over_experts(r_s), ALU.is_equal))

            def route_first():
                dve.wait_ge(s["consts"], 7)
                pick(first_e, prob_e)
                link(dve.scalar_tensor_tensor(r_c[:, :, :], first_e[:, :, :], -NEVER, prob_e[:, :, :], ALU.mult, ALU.add))

            def route_second():
                pick(r_a, r_c)
                link(dve.tensor_tensor(r_b[:, :, :], r_a[:, :, :], first_e[:, :, :], ALU.add))
                link(dve.tensor_tensor(mix[:, :, 0:NR], r_b[:, :, :], prob_e[:, :, :], ALU.mult))

            def route_gate():
                link(dve.tensor_scalar(r_s[:, :], gate_e[:, :], 1.0, None, ALU.add))
                link(dve.reciprocal(mix[:, :, NR], r_s[:, :]))
                dve.tensor_scalar(mix[:, :, :], mix[:, :, :], tanh_g[:, 1:2], 1.0 / (PROJ_SCALE * W_SCALE), ALU.mult,
                                  ALU.mult).then_inc(s["mix_done"], 1)

            def combine(at, e, tiles, bank):
                dve.wait_ge(s["down_done"], at + 1)
                for i, t in enumerate(tiles):
                    last = dve.scalar_tensor_tensor(x_mid[:, t, :], bank[:, i * P:(i + 1) * P],
                                                    mix[:, t, bass.ds(e, 1)], x_mid[:, t, :], ALU.mult, ALU.add)
                last.then_inc(s["summed"], 1)

            def expert(e, par, first, last):
                second = isinstance(e, int) and e == 1
                for c in range(4):
                    C = 4 * e + c
                    dve.wait_ge(s["silu_done"], C + 1)
                    if not first:
                        dve.wait_ge(s["hid_lo_done"], C - 3)
                    dve.tensor_tensor(hid[:, c, :], GU_BANKS[GU_SLOT[par][c]][1][:, :], silu[:, c % 2, :],
                                      ALU.mult).then_inc(s["hid_done"], 1)
                    if first and c == 0:
                        low_x(1, 3)
                    if first and c == 1:
                        route_logits()
                    if not first and not last and c >= 2:
                        if second and c == 2:
                            dve.wait_ge(s["mix_done"], 1)
                        combine(2 * e - 2 + c - 2, e - 1, range(4 * c - 8, 4 * c - 4), misc[c - 2])
                    if c == 1 and not first and not last:
                        low_gate_up(e + 1, 1 - par)
                    if first and c == 2:
                        route_softmax()
                    if c == 3 and not first and not last:
                        low_down(e + 1, 1 - par)
                    if first and c == 3:
                        route_first()
                    if second and c == 0:
                        route_second()
                    if second and c == 1:
                        route_gate()

            loop_experts(dve, expert)
            for h in range(2):
                combine(2 * NE - 4 + h, NE - 2, range(4 * h, 4 * h + 4), misc[h])
            for part, (tiles, bank) in enumerate(LAST_DOWN):
                combine(2 * NE - 2 + part, NE - 1, tiles, bank)

        @block.tensor
        def _(pe):
            def three(out_ap, lhs_hi, lhs_lo, rhs_hi, rhs_lo, start=True, stop=True):
                pe.matmul(out_ap, lhs_hi, rhs_hi, start=start, stop=False)
                pe.matmul(out_ap, lhs_hi, rhs_lo, start=False, stop=False)
                return pe.matmul(out_ap, lhs_lo, rhs_hi, start=False, stop=stop)

            def turn_x(half, at):
                for j in range(4):
                    pe.wait_ge(s["normed"], 4 * at + j + 1)
                    last = pe.transpose((outs if at < 2 else misc)[half][:, j * P:(j + 1) * P], x_norm[:, 4 * half + j, :], ident[:, :])
                last.then_inc(s["transposed"], 1)

            def project(hp1, par1, j, g, first):
                if j == 0:
                    pe.wait_ge(s["w_done"], hp1 + 1)
                if first:
                    if j >= 4:
                        pe.wait_ge(s["lo_done"], j - 3)
                elif j >= 8:
                    pe.wait_ge(s["v_done"], 4 * hp1 + j - 7)
                elif j >= 2:
                    pe.wait_ge(s["lo_done"], 6 * hp1 + j - 1)
                else:
                    pe.wait_ge(s["v_done"], 4 * hp1 + j - 1)
                out_ap = group_bank(j, first)
                if g < 2:
                    cols = slice(g * 512, (g + 1) * 512)
                    last = three(out_ap[:, :], w_hi[:, par1, 0:P], w_lo[:, par1, 0:P], xT_hi[:, cols], xT_lo[:, cols])
                elif g < 6:
                    if first:
                        pe.wait_ge(s["ctx_done"], g - 1)
                    cols = slice((g - 2) * 512, (g - 1) * 512)
                    last = three(out_ap[:, :], w_hi[:, par1, P:2 * P], w_lo[:, par1, P:2 * P], ctx_hi[:, cols], ctx_lo[:, cols])
                else:
                    for kt in range(KT):
                        cols = slice(((g - 6) * KT + kt) * P, ((g - 6) * KT + kt + 1) * P)
                        last = three(out_ap[:, kt * P:(kt + 1) * P], ctx_hi[:, cols], ctx_lo[:, cols],
                                     w_hi[:, par1, 2 * P:3 * P], w_lo[:, par1, 2 * P:3 * P])
                last.then_inc(s["projected"], 1)

            def near_scores(u, par, qt):
                n, h = u // 2, u % 2
                cols = slice(n * L + qt * P, n * L + (qt + 1) * P)
                pe.matmul(near[qt][:, :], q_twice[:, par, h, cols], k_both[:, par, h, n * S:(n + 1) * S],
                          start=True, stop=True).then_inc(s["near_done"], 1)

            def turn_max(U, u, qt):
                pe.wait_ge(s["max_done"], 2 * U + qt + 1)
                pe.matmul(near[qt][:, 0:P], max_cols[:, u % 2, qt, :], neg_ident[:, :], start=True,
                          stop=True).then_inc(s["shift_made"], 1)

            def scores(U, u, par, half):
                n, h = u // 2, u % 2
                qs = slice(n * L, (n + 1) * L)
                for j in range(2):
                    kt = 2 * half + j
                    ks = slice(n * S + kt * P, n * S + (kt + 1) * P)
                    pe.matmul(score[half][:, j * L:(j + 1) * L], k_both[:, par, h, ks], q_twice[:, par, h, qs],
                              start=True, stop=False)
                    last = pe.matmul(score[half][:, j * L:(j + 1) * L], k_row[0:D + 1, par, h, ks],
                                     q_row[0:D + 1, par, h, qs],
                                     start=False, stop=True)
                last.then_inc(s["scores_done"], 1)

            def weigh_values(m, n, vpar, kt, guard):
                bank = outs[n % 2]
                if kt == 0:
                    pe.wait_ge(s["probs_done"], 4 * m + 4)
                    pe.wait_ge(s["v_done"], m + 1)
                    if guard:
                        pe.wait_ge(s["psum_read"], m - 1)
                for h in range(2):
                    last = pe.matmul(bank[D * h:D * h + D, 0:L], v_sb[:, vpar, n * KT + kt, D * h:D * h + D],
                                     probs[:, n % 2 * 2 + h, kt * L:(kt + 1) * L], start=(kt == 0), stop=(kt == 3))
                if kt == 3:
                    last.then_inc(s["values_done"], 1)

            def sum_probs(m, n):
                bank = outs[n % 2]
                pe.wait_ge(s["sum_hi_done"], m + 1)
                for h in range(2):
                    pe.matmul(bank[D * h:D * h + D, L:2 * L], ones16[:, :], sum_hi[:, n % 2 * 2 + h, :],
                              start=True, stop=False)
                pe.wait_ge(s["sum_lo_done"], m + 1)
                for h in range(2):
                    last = pe.matmul(bank[D * h:D * h + D, L:2 * L], ones16[:, :], sum_lo[:, n % 2 * 2 + h, :],
                                     start=False, stop=True)
                last.then_inc(s["pv_done"], 1)

            def project_out(t, hp0, hp1):
                cols = slice(t * P, (t + 1) * P)
                for hp in range(hp0, hp1):
                    if hp == HP - 1:
                        pe.wait_ge(s["oT_done"], 4 * hp + t // QT + 1)
                    last = three(OUT_BANKS[t // 2][:, (t % 2) * P:(t % 2 + 1) * P], oT_hi[:, hp, cols], oT_lo[:, hp, cols],
                                 wo_hi[:, hp, :], wo_lo[:, hp, :], start=(hp == 0 and t % 2 == 0),
                                 stop=(hp == HP - 1 and t % 2 == 1))
                if hp1 == HP and t % 2 == 1:
                    last.then_inc(s["y_done"], 1)

            pe.wait_ge(s["consts"], 1)

            def keep_busy(times):
                for _ in range(times):
                    pe.transpose(near[0][:, 0:P], ident[:, :], ident[:, :])

            keep_busy(22)
            turn_x(0, 0)
            keep_busy(7)
            pe.wait_ge(s["ctx_done"], 1)
            project(0, 0, 0, FIRST_ORDER[0], True)
            pe.wait_ge(s["xT_done"], 1)
            for j in range(1, 3):
                project(0, 0, j, FIRST_ORDER[j], True)
            keep_busy(18)
            project(0, 0, 3, FIRST_ORDER[3], True)
            keep_busy(8)
            turn_x(1, 1)
            keep_busy(3)
            project(0, 0, 4, FIRST_ORDER[4], True)
            pe.wait_ge(s["xT_done"], 2)
            project(0, 0, 5, FIRST_ORDER[5], True)
            pe.wait_ge(s["start_near0"], 64)
            for qt in range(QT):
                near_scores(0, 0, qt)
            for j in range(6, 8):
                project(0, 0, j, FIRST_ORDER[j], True)
            pe.wait_ge(s["consts"], 6)
            pe.wait_ge(s["start_near1"], 64)
            for qt in range(QT):
                turn_max(0, 0, qt)
                project(0, 0, 8 + qt, FIRST_ORDER[8 + qt], True)
                pe.wait_ge(s["shift_done"], qt + 1)
                near_scores(1, 0, qt)
            pe.wait_ge(s["bias_prod"], 4)
            pe.wait_ge(s["bo_loaded"], 16)
            pe.matmul(outs[0][:, 0:P], ones[:, :], bvw[:, 0, :], start=True, stop=False)
            pe.matmul(outs[0][:, 0:P], ones[0:1, :], bo_row[:, :], start=False, stop=True).then_inc(s["bias_sum"], 1)
            turn_max(1, 1, 0)
            pe.wait_ge(s["v_done"], 2)

            def body(hp, par, first, last):
                for u in range(UN):
                    U, n, h = hp * UN + u, u // 2, u % 2
                    for half in range(2):
                        if half == 0:
                            pe.wait_ge(s["shift_done"], 2 * U + 2)
                        if not first or u >= 1:
                            pe.wait_ge(s["probs_done"], 2 * U + half - 1)
                        if half == 0 and (u == 0 and not first or first and u == 2):
                            pe.wait_ge(s["row_moved"], 32 * hp + 32)
                        if first and u == 4 and half == 0:
                            pe.wait_ge(s["rest_q_row"], 32)
                        if first and u < 2 and half == 0:
                            pe.wait_ge(s[f"start_row{u}"], 32)
                        scores(U, u, par, half)
                        if not last and (u, half) in GROUP:
                            project(hp + 1, 1 - par, GROUP[u, half], GROUP[u, half], False)
                        if n >= 1:
                            if first and n == 1 and (h, half) == (0, 0):
                                pe.wait_ge(s["bias_out_done"], 1)
                            weigh_values(4 * hp + n - 1, n - 1, par, 2 * h + half, not first or n >= 3)
                        elif not first:
                            weigh_values(4 * hp + n - 1, NB - 1, 1 - par, 2 * h + half, True)
                        if (h, half) == (0, 1) and (not first or n >= 2):
                            sum_probs(4 * hp + n - 2, n % 2)
                        if last and u >= 1:
                            if (u, half) == (1, 0):
                                pe.wait_ge(s["v_done"], 4 * HP)
                                pe.wait_ge(s["wo_done"], 1)
                                pe.wait_ge(s["oT_done"], 4 * (HP - 2) + 2)
                            for i in range(2 * (2 * u + half - 2), 2 * (2 * u + half - 1)):
                                project_out(i // (HP - 1), i % (HP - 1), i % (HP - 1) + 1)
                        if not (last and u >= UN - 2):
                            pe.wait_ge(s["shift_done"], 2 * U + half + 3)
                            if u == UN - 2 and half == 0:
                                pe.wait_ge(s["q_moved"], 96 * hp + 96)
                                pe.wait_ge(s["k0_moved"], 32 * hp + 64)
                            if u == UN - 1 and half == 0:
                                pe.wait_ge(s["k1_moved"], 32 * hp + 64)
                            if first and half == 0:
                                if u < 2:
                                    pe.wait_ge(s[f"k{u}_moved"], 32)
                                if u in (2, 3):
                                    pe.wait_ge(s[f"rest_q{u - 2}"], 32)
                            near_scores((u + 2) % UN, par if u < UN - 2 else 1 - par, half)
                        if half == 0:
                            if not (last and u == UN - 1):
                                turn_max(U + 1, (u + 1) % UN, 1)
                        elif not (last and u >= UN - 2):
                            turn_max(U + 2, (u + 2) % UN, 0)

            loop_pairs(pe, body)
            for t in range(2):
                project_out(t, HP - 1, HP)
            sum_probs(4 * HP - 2, 0)
            for kt in range(KT):
                weigh_values(4 * HP - 1, NB - 1, 1, kt, True)
            for t in range(2, 4):
                project_out(t, HP - 1, HP)
            project_out(4, 0, HP - 1)
            sum_probs(4 * HP - 1, 1)
            project_out(5, 0, HP - 1)
            for t in range(4, 6):
                project_out(t, HP - 1, HP)
            for t in range(6, 8):
                project_out(t, 0, HP - 1)
            for t in range(6, 8):
                project_out(t, HP - 1, HP)
            turn_x(0, 2)

            def make_logits(half):
                if half == 0:
                    pe.wait_ge(s["router_done"], 1)
                else:
                    pe.wait_ge(s["xT_done"], 4)
                for t in range(4 * half, 4 * half + 4):
                    cols = slice(t * P, (t + 1) * P)
                    last = three(misc[0][:, 16 * t:16 * t + NE], xT_hi[:, cols], xT_lo[:, cols], router_hi[:, :], router_lo[:, :])
                last.then_inc(s["logits_done"], 1)

            def gate_up(e, C, c, par, first):
                tc, ft = c // 2, c % 2
                if c == 0:
                    pe.wait_ge(s["wf_done"], 2 * e + 1)
                    if first:
                        pe.wait_ge(s["xT_done"], 3)
                if not first or c >= GU_BACK[c]:
                    pe.wait_ge(s["hid_done"], C - GU_BACK[c] + 1)
                if first and c == 1:
                    pe.wait_ge(s["attn_done"], 4)
                gate_bank, up_bank = GU_BANKS[GU_SLOT[par][c]]
                cols = slice(tc * 512, (tc + 1) * 512)
                g = slice(ft * P, (ft + 1) * P)
                u = slice((FT + ft) * P, (FT + ft + 1) * P)
                three(gate_bank[:, :], wf_hi[:, par, g], wf_lo[:, par, g], xT_hi[:, cols], xT_lo[:, cols])
                three(up_bank[:, :], wf_hi[:, par, u], wf_lo[:, par, u], xT_hi[:, cols],
                      xT_lo[:, cols]).then_inc(s["gu_done"], 1)

            def down_tiles(par, tiles, bank):
                for i, t in enumerate(tiles):
                    cols = slice(t * P, (t + 1) * P)
                    for ft in range(FT):
                        d = slice((2 * FT + ft) * P, (2 * FT + ft + 1) * P)
                        last = three(bank[:, i * P:(i + 1) * P], hid_hi[:, par, ft, cols], hid_lo[:, par, ft, cols],
                                     wf_hi[:, par, d], wf_lo[:, par, d], start=(ft == 0), stop=(ft == FT - 1))
                last.then_inc(s["down_done"], 1)

            def down(e, par, yb, first):
                if yb == 0:
                    pe.wait_ge(s["wf_done"], 2 * e + 2)
                pe.wait_ge(s["hid_lo_done"], 4 * e + 2 * yb + 2)
                if not first:
                    pe.wait_ge(s["summed"], 2 * e - 1 + yb)
                down_tiles(par, range(4 * yb, 4 * yb + 4), misc[yb])

            def expert(e, par, first, last):
                second = not first and isinstance(e, int) and e == 1
                for c in range(4):
                    gate_up(e, 4 * e + c, c, par, first)
                    if c == 1 and first:
                        make_logits(0)
                        turn_x(1, 3)
                        make_logits(1)
                    if c in (1, 2) and not first and not last:
                        down(e - 1, 1 - par, c - 1, second)

            loop_experts(pe, expert)
            down(NE - 2, 1, 0, False)
            down(NE - 2, 1, 1, False)
            down(NE - 1, 0, 0, False)
            pe.wait_ge(s["hid_lo_done"], 4 * NE)
            pe.wait_ge(s["summed"], 2 * NE - 2)
            for tiles, bank in LAST_DOWN[1:]:
                down_tiles(0, tiles, bank)


def kernel(x, ctx_1024, g_xattn, g_ffn, L0_xattn_Wq, L0_xattn_bq, L0_xattn_Wk, L0_xattn_bk, L0_xattn_Wv,
           L0_xattn_bv, L0_xattn_Wo, L0_xattn_bo, L0_ffn_router_w, L0_ffn_w_gate, L0_ffn_w_up, L0_ffn_w_down,
           L0_ffn_sw_gate, L0_ffn_sw_up, L0_ffn_sw_down, L0_ffn_gate_w):
    import numpy as np
    import concourse.bacc as bacc
    from concourse import mybir as mb
    from concourse.bass_utils import run_bass_kernel_spmd

    a = np.asarray
    x, c = a(x), a(ctx_1024)
    B, Lq, Em = x.shape
    pairs = L0_xattn_Wq.shape[0] // 128
    gate = np.concatenate([a(L0_ffn_w_gate), a(L0_ffn_sw_gate)[None]])
    up = np.concatenate([a(L0_ffn_w_up), a(L0_ffn_sw_up)[None]])
    down = np.concatenate([a(L0_ffn_w_down), a(L0_ffn_sw_down)[None]])
    n_e, F, _ = down.shape
    down = down.reshape(n_e, F // 128, 128, Em).transpose(0, 2, 1, 3).reshape(n_e, 128, -1)
    wqkv = np.stack([a(w).reshape(pairs, 128, Em).transpose(2, 0, 1) for w in (L0_xattn_Wq, L0_xattn_Wk, L0_xattn_Wv)], axis=2)
    data = {
        "xs": x.reshape(B * Lq, Em),
        "ctxT": c.reshape(-1, Em).T,
        "small": np.concatenate([
            np.broadcast_to(a(g_xattn).reshape(1, 1), (128, 1)), np.broadcast_to(a(g_ffn).reshape(1, 1), (128, 1)),
            np.stack([a(L0_xattn_bq).reshape(pairs, 128).T, a(L0_xattn_bk).reshape(pairs, 128).T], axis=2).reshape(128, -1),
            a(L0_xattn_bv).reshape(pairs, 128).T, np.concatenate([a(L0_ffn_router_w), a(L0_ffn_gate_w)]).T], axis=1),
        "wqkv": wqkv.reshape(Em, pairs, 3 * 128),
        "woT": a(L0_xattn_Wo).T,
        "bo": a(L0_xattn_bo).reshape(1, Em),
        "wffn": np.concatenate([gate, up, down], axis=2),
    }
    nc = bacc.Bacc("TRN2", target_bir_lowering=False, num_devices=1)
    arrays, args = {}, {}
    for name, value in data.items():
        value = np.ascontiguousarray(value)
        arrays[name] = value
        args[name] = nc.dram_tensor(name, value.shape, mb.dt.from_np(value.dtype), kind="ExternalInput").ap()
    y = nc.dram_tensor("y", (B * Lq, Em), mb.dt.float32, kind="ExternalOutput").ap()
    flamingo_block(nc, out=y, **args)
    result = run_bass_kernel_spmd(nc, [arrays], core_ids=[0])
    return result.results[0]["y"].reshape(B, Lq, Em)
```
